# Optimizing a Trainium2 kernel written in Bass

```python
import numpy as np
import jax
import jax.numpy as jnp

def _softmax(x, axis=-1):
    return jax.nn.softmax(x, axis=axis)

def _gelu(x):
    return jax.nn.gelu(x, approximate=True)

def _silu(x):
    return jax.nn.silu(x)

def _sigmoid(x):
    return jax.nn.sigmoid(x)

def _layernorm(x, axis=-1, eps=1e-05):
    m = jnp.mean(x, axis=axis, keepdims=True)
    v = jnp.var(x, axis=axis, keepdims=True)
    return (x - m) / jnp.sqrt(v + eps)

def _scatter_add(tgt, idx, src, axis=0):
    return tgt.at[idx].add(src)

def _segment_sum(src, seg, n):
    return jax.ops.segment_sum(src, seg, n)
kernel_name = 'mk_flamingo_gated_d1_seqx_r4_7d5304'

def setup_inputs(seed: int=0):
    np.random.seed(seed)
    _w = jnp.asarray

    def _rec_inputs():
        import jax
        import jax.numpy as jnp
        _rk = jax.random.key(seed)
        x = -0.0002928 + 1 * jax.random.normal(jax.random.fold_in(_rk, 1), (16, 128, 256), jnp.float32)
        _lenS = 128 - jax.random.randint(jax.random.fold_in(_rk, 7), (16,), 0, max(1, 128 // 4) + 1, jnp.int32)
        _lenS2 = 128 - jax.random.randint(jax.random.fold_in(_rk, 8), (16,), 0, max(1, 128 // 4) + 1, jnp.int32)
        _ctx_1024P = jax.random.normal(jax.random.fold_in(_rk, 11), (16, 16, 256), jnp.float32)
        _ctx_1024c = jax.random.dirichlet(jax.random.fold_in(_rk, 511), 0.3 * jnp.ones((16,), jnp.float32), (16, 128))
        _ctx_1024t = jnp.einsum('bsk,bkd->bsd', _ctx_1024c, _ctx_1024P)
        _ctx_1024t = _ctx_1024t * jax.lax.rsqrt(jnp.mean(jnp.square(_ctx_1024t)) + 1e-12) * 0.953939
        ctx_1024 = -1.39393e-06 + 0.999914 * (_ctx_1024t + 0.3 * jax.random.normal(jax.random.fold_in(_rk, 611), (16, 128, 256), jnp.float32))
        _g = jax.random.normal(jax.random.fold_in(_rk, 9001), (2, 1), jnp.float32)
        _g = jnp.sign(_g) * jnp.maximum(jnp.abs(_g), 1.0) + (_g == 0) * 1.0
        g_xattn = _g[0]
        g_ffn = _g[1]
        return (x, ctx_1024, g_xattn, g_ffn)
    x, ctx_1024, g_xattn, g_ffn = _rec_inputs()

    def _L0_xattn_setup():
        import jax, jax.numpy as jnp
        import numpy as np
        NUM_HEADS = 16
        key = jax.random.key(seed)
        ks = jax.random.split(key, 8)
        B, S, E = (2, 512, 256)
        std = 0.02
        return {'q': jax.random.normal(ks[0], (B, S, E), dtype=jnp.float32), 'k': jax.random.normal(ks[1], (B, S, E), dtype=jnp.float32), 'v': jax.random.normal(ks[2], (B, S, E), dtype=jnp.float32), 'Wq': jax.random.normal(ks[3], (E, E), dtype=jnp.float32) * std, 'Wk': jax.random.normal(ks[4], (E, E), dtype=jnp.float32) * std, 'Wv': jax.random.normal(ks[5], (E, E), dtype=jnp.float32) * std, 'Wo': jax.random.normal(ks[6], (E, E), dtype=jnp.float32) * std, 'bo': jnp.zeros((E,), dtype=jnp.float32)}
    _L0_xattn_all = _L0_xattn_setup()
    _L0_xattn_in = {k: v for k, v in _L0_xattn_all.items() if k in ('Wq', 'Wk', 'Wv', 'Wo', 'bo')}
    del _L0_xattn_all

    def _L0_ffn_setup():
        import jax, jax.numpy as jnp
        import numpy as np
        DM = 256
        NEXPERTS = 32
        EXPERTSETS = 4
        EXPERTSIZE = 32
        BATCH, SEQ = (4, 512)
        key = jax.random.key(seed)
        k0, k1, k2, k3 = jax.random.split(key, 4)
        scale = 0.02
        x = jax.random.normal(k0, (BATCH, SEQ, DM), jnp.float32)
        controller = jax.random.normal(k1, (DM, NEXPERTS, EXPERTSETS), jnp.float32) * scale
        f1 = jax.random.normal(k2, (DM, NEXPERTS, EXPERTSETS, EXPERTSIZE), jnp.float32) * scale
        bias = jnp.zeros((NEXPERTS, EXPERTSETS, EXPERTSIZE), jnp.float32)
        f2 = jax.random.normal(k3, (NEXPERTS, EXPERTSETS, EXPERTSIZE, DM), jnp.float32) * scale
        return {'x': x, 'controller': controller, 'f1': f1, 'bias': bias, 'f2': f2}
    _L0_ffn_all = _L0_ffn_setup()
    _L0_ffn_in = {k: v for k, v in _L0_ffn_all.items() if k in ('controller', 'f1', 'bias', 'f2')}
    del _L0_ffn_all
    return {'x': x, 'ctx_1024': ctx_1024, 'g_xattn': g_xattn, 'g_ffn': g_ffn, 'L0_xattn_Wq': _L0_xattn_in['Wq'], 'L0_xattn_Wk': _L0_xattn_in['Wk'], 'L0_xattn_Wv': _L0_xattn_in['Wv'], 'L0_xattn_Wo': _L0_xattn_in['Wo'], 'L0_xattn_bo': _L0_xattn_in['bo'], 'L0_ffn_controller': _L0_ffn_in['controller'], 'L0_ffn_f1': _L0_ffn_in['f1'], 'L0_ffn_bias': _L0_ffn_in['bias'], 'L0_ffn_f2': _L0_ffn_in['f2']}

def reference(x, ctx_1024, g_xattn, g_ffn, L0_xattn_Wq, L0_xattn_Wk, L0_xattn_Wv, L0_xattn_Wo, L0_xattn_bo, L0_ffn_controller, L0_ffn_f1, L0_ffn_bias, L0_ffn_f2):
    import jax
    import jax.numpy as jnp

    def _L0_xattn_ref(q, k, v, Wq, Wk, Wv, Wo, bo):
        import jax, jax.numpy as jnp
        import numpy as np
        NUM_HEADS = 16
        B, S, E = q.shape
        H = NUM_HEADS
        D = E // H
        Q = (q @ Wq.T).reshape(B, S, H, D).transpose(0, 2, 1, 3)
        K = (k @ Wk.T).reshape(B, S, H, D).transpose(0, 2, 1, 3)
        V = (v @ Wv.T).reshape(B, S, H, D).transpose(0, 2, 1, 3)
        scores = jnp.einsum('bhsd,bhtd->bhst', Q, K)
        causal = jnp.tril(jnp.ones((S, S), dtype=bool))
        scores = jnp.where(causal, scores, -jnp.inf)
        scores = scores / np.sqrt(D).astype(np.float32)
        attn = jax.nn.softmax(scores, axis=-1)
        out = jnp.einsum('bhst,bhtd->bhsd', attn, V)
        out = out.transpose(0, 2, 1, 3).reshape(B, S, E)
        return out @ Wo.T + bo

    def _L0_ffn_ref(x, controller, f1, bias, f2):
        import jax, jax.numpy as jnp
        import numpy as np
        DM = 256
        NEXPERTS = 32
        EXPERTSETS = 4
        EXPERTSIZE = 32
        BATCH, SEQ = (4, 512)
        B, L, d = x.shape
        t = controller.shape[1]
        g = L // t
        grouped = x.reshape(B, g, t, d)
        logits = jnp.einsum('bgtd,des->bgtes', grouped, controller)
        tie = jnp.linspace(0.0, 1e-06, t, dtype=logits.dtype).reshape(t, 1, 1)
        logits = logits + tie
        perm = (logits == jnp.max(logits, axis=-3, keepdims=True)).astype(x.dtype)
        perm = jax.lax.stop_gradient(perm)
        dispatched = jnp.einsum('bgtd,bgtes->bgesd', grouped, perm)
        inner = jax.nn.relu(jnp.einsum('bgesd,desf->bgesf', dispatched, f1) + bias)
        intermediate = jnp.einsum('bgesf,esfd->bgesd', inner, f2)
        out = jnp.einsum('bgesd,bgtes->bgtd', intermediate, perm)
        return out.reshape(B, L, d)
    x = x + jnp.tanh(g_xattn[0]) * _L0_xattn_ref(_layernorm(x, axis=-1), ctx_1024, ctx_1024, L0_xattn_Wq, L0_xattn_Wk, L0_xattn_Wv, L0_xattn_Wo, L0_xattn_bo)
    x = x + jnp.tanh(g_ffn[0]) * _L0_ffn_ref(_layernorm(x, axis=-1), L0_ffn_controller, L0_ffn_f1, L0_ffn_bias, L0_ffn_f2)
    return x

_drawn_inputs = setup_inputs


def setup_inputs(seed=0):
    import zlib

    import numpy as np

    out = dict(_drawn_inputs(seed))
    spreads = {'L0_xattn_bo': (0.0, 0.1), 'L0_ffn_bias': (0.0, 0.553)}
    factors = {'L0_xattn_Wq': 8.0, 'L0_xattn_Wk': 8.0}
    for name, (base, spread) in spreads.items():
        noise = np.random.default_rng([zlib.crc32(name.encode()), seed]).standard_normal(out[name].shape)
        drawn = base * np.exp(spread * noise) if base else spread * noise
        out[name] = jnp.asarray(drawn.astype(out[name].dtype))
    for name, factor in factors.items():
        out[name] = (out[name] * factor).astype(out[name].dtype)
    return out
```

```python
from contextlib import ExitStack

import concourse.bass as bass
from concourse import mybir

F32 = mybir.dt.float32
BF16 = mybir.dt.bfloat16
ALU = mybir.AluOpType
ACT = mybir.ActivationFunctionType
AX_X = mybir.AxisListType.X

P = 128
NB = 16
E = 256
KH = E // P
H = 16
D = E // H
HC = 4
NC = H // HC
DP = 32
NE, NS, F = 32, 4, 32
SLOTS = NE * NS
T = 32
NG = P // T
GROUPS = NB * NG
RING = 4
XC = 4
EPS = 1e-5
NEG = -(2.0 ** 100)


def build(nc, x, ctxT, wattn, bo, gates, ctrl, wexp, ebias, constf, out):
    with ExitStack() as ctx:
        def sb(name, shape, dt=F32):
            return ctx.enter_context(nc.sbuf_tensor(name, shape, dt))

        def sem(name):
            return ctx.enter_context(nc.semaphore(name))

        bank = [ctx.enter_context(nc.psum_tensor(f"bank{i}", [P, 512], F32)) for i in range(8)]

        cf = sb("cf", [P, P + HC + P + NG + P])
        ident = cf[:, 0:P]
        headmask = cf[:, P:P + HC]
        tie = cf[:, P + HC:P + HC + P]
        groupmask = cf[:, P + HC + P:P + HC + P + NG]
        mask = cf[:, P + HC + P + NG:P + HC + P + NG + P]
        cb = sb("cb", [P, P + HC * P], BF16)
        identb = cb[:, 0:P]
        causal = cb[:, P:P + HC * P]
        w = sb("w", [P, 4, KH, E])
        wk, wq, wv, wo = (w[:, i] for i in range(4))
        bo_sb = sb("bo_sb", [P, E])
        gates_sb = sb("gates_sb", [P, 2])
        tg = sb("tg", [P, 2])
        ctrl_sb = sb("ctrl_sb", [P, KH, SLOTS])
        ebias_sb = sb("ebias_sb", [P, NE])

        xs = sb("xs", [P, NB, E])
        stats = sb("stats", [P, NB, 6])
        mv = sb("mv", [P, NB, 2])
        ve = sb("ve", [P, NB])
        sd = sb("sd", [P, NB])
        rs = sb("rs", [P, NB])
        nt = sb("nt", [P, NB])
        xn = sb("xn", [P, 4, E])
        xT = sb("xT", [P, KH, P])
        cT = sb("cT", [P, 2, KH, P])
        kd = sb("kd", [P, 2, KH, HC, P])
        qz = sb("qz", [P, 2, KH, 2, P])
        va = sb("va", [P, 2, H, DP])
        nmax = sb("nmax", [P, H])
        pr = sb("pr", [P, 2, HC, P])
        pT = sb("pT", [P, 2, HC * P])
        oT = sb("oT", [P, NC * P])
        rsum = sb("rsum", [P, H])
        on = sb("on", [P, E])
        onT = sb("onT", [P, KH, P])

        lt = sb("lt", [P, P])
        gmax = sb("gmax", [P, NG])
        pc = sb("pc", [P, 2, P])
        permT = sb("permT", [P, NB, P])
        permb = sb("permb", [P, NG, P])
        routed = sb("routed", [P, KH, GROUPS, SLOTS])
        wx = sb("wx", [P, RING, KH * P + E])
        xe = sb("xe", [P, 2, KH, NS, GROUPS])
        hb = sb("hb", [P, 2, NS, GROUPS])
        yg = sb("yg", [P, 2, KH, NG, SLOTS])
        pg = sb("pg", [P, 2, P])
        ys = sb("ys", [P, 2, NG, E])
        yo = sb("yo", [P, 2, E])

        x_loaded = [sem(f"x_loaded{i}") for i in range(NB // XC)]
        consts_loaded = sem("consts_loaded")
        maskb_ready = sem("maskb_ready")
        small_loaded = sem("small_loaded")
        gates_loaded = sem("gates_loaded")
        w_loaded = [sem(f"w_loaded{i}") for i in range(4)]
        ctx_loaded = [sem(f"ctx_loaded{i}") for i in range(2)]
        wx_loaded = [sem(f"wx_loaded{i}") for i in range(RING)]
        stored = [sem(f"stored{i}") for i in range(2)]
        zeroed = sem("zeroed")
        stats_ready = sem("stats_ready")
        var_ready = sem("var_ready")
        sd_ready = sem("sd_ready")
        rs_step = sem("rs_step")
        mom_step = sem("mom_step")
        tanh_ready = sem("tanh_ready")
        bo_ready = sem("bo_ready")
        xn_ready = sem("xn_ready")
        xT_done = sem("xT_done")
        xT_ready = sem("xT_ready")
        k_done = sem("k_done")
        k_ready = sem("k_ready")
        q_done = sem("q_done")
        q_ready = sem("q_ready")
        v_done = sem("v_done")
        v_ready = sem("v_ready")
        oT_ready = sem("oT_ready")
        o_done = sem("o_done")
        rsum_ready = sem("rsum_ready")
        on_ready = sem("on_ready")
        onT_done = sem("onT_done")
        onT_ready = sem("onT_ready")
        y_done = sem("y_done")
        xb_ready = sem("xb_ready")
        x1_ready = sem("x1_ready")
        s_done = sem("s_done")
        max_ready = sem("max_ready")
        p_ready = sem("p_ready")
        pT_done = sem("pT_done")
        pT_ready = sem("pT_ready")
        av_done = sem("av_done")
        rn_ready = sem("rn_ready")
        rT_done = sem("rT_done")
        rT_ready = sem("rT_ready")
        lg_done = sem("lg_done")
        lt_ready = sem("lt_ready")
        gmax_ready = sem("gmax_ready")
        perm_ready = sem("perm_ready")
        pm_done = sem("pm_done")
        pm_ready = sem("pm_ready")
        d_done0 = sem("d_done0")
        d_done1 = sem("d_done1")
        d_kept0 = sem("d_kept0")
        d_kept1 = sem("d_kept1")
        xe_ready = sem("xe_ready")
        h_done = sem("h_done")
        h_ready = sem("h_ready")
        e_done = sem("e_done")
        e_kept = sem("e_kept")
        permT_kept = sem("permT_kept")
        yg_ready = sem("yg_ready")
        pg_ready = sem("pg_ready")
        yT_done = sem("yT_done")
        ys_ready = sem("ys_ready")
        c_done = sem("c_done")
        yo_ready = sem("yo_ready")

        BS, BT, BO, BX, BK, BQ, BY = bank[0:2], bank[2], bank[3], bank[4], bank[5], bank[6], bank[7]

        block = ctx.enter_context(nc.Block())

        @block.sync
        def _(sp):
            sp.dma_start(xs[:, 0:XC, :], x[0:XC].rearrange("b s e -> s b e")).then_inc(x_loaded[0], 16)
            sp.dma_start(cT[:, 0], ctxT[0]).then_inc(ctx_loaded[0], 16)
            for i in range(1, NB // XC):
                sp.dma_start(xs[:, i * XC:(i + 1) * XC, :],
                             x[i * XC:(i + 1) * XC].rearrange("b s e -> s b e")).then_inc(x_loaded[i], 16)
            sp.dma_start(cT[:, 1], ctxT[1]).then_inc(ctx_loaded[1], 16)
            sp.dma_start(ctrl_sb[:, :, :], ctrl).then_inc(small_loaded, 16)
            sp.dma_start(ebias_sb[:, :], ebias).then_inc(small_loaded, 16)
            for r in range(RING):
                sp.dma_start(wx[:, r], wexp[r]).then_inc(wx_loaded[r], 16)
            with sp.Fori(1, NB // 2) as i:
                b = i * 2
                for k in range(2):
                    sp.wait_ge(v_done, b + (k - 1))
                    sp.dma_start(cT[:, k], ctxT[b + k]).then_inc(ctx_loaded[k], 16)
            with sp.Fori(1, NE // RING) as i:
                e = i * RING
                for r in range(RING):
                    sp.wait_ge(e_done, e + (r - RING + 1))
                    sp.dma_start(wx[:, r], wexp[e + r]).then_inc(wx_loaded[r], 16)
            with sp.Fori(0, NB // 2) as i:
                b = i * 2
                for k in range(2):
                    sp.wait_ge(yo_ready, b + (k + 1))
                    sp.dma_start(out[b + k], yo[:, k]).then_inc(stored[k], 16)
            for k in range(2):
                sp.wait_ge(stored[k], 16 * (NB // 2))


        @block.gpsimd
        def _(pool):
            pool.memset(qz[:, :, :, :, :], 0.0).then_inc(zeroed, 1)
            pool.memset(va[:, :, :, :], 1.0).then_inc(zeroed, 1)
            pool.memset(hb[:, :, :, :], 0.0).then_inc(zeroed, 1)
            pool.wait_ge(consts_loaded, 16)
            pool.tensor_copy(identb, ident).then_inc(maskb_ready, 1)
            for j in range(HC):
                pool.tensor_copy(causal[:, j * P:(j + 1) * P], mask).then_inc(maskb_ready, 1)
            pool.wait_ge(bo_ready, 1)
            with pool.Fori(0, NB) as b:
                pool.wait_ge(xn_ready, b + 1)
                pool.tensor_tensor(xs[:, b, :], xs[:, b, :], bo_sb[:, :], ALU.add).then_inc(xb_ready, 1)
            with pool.Fori(0, NB // 2) as i:
                b = i * 2
                for k in range(2):
                    pool.wait_ge(perm_ready, b + (k + 1))
                    pool.tensor_copy(permT[:, b + k, :], pc[:, k, :]).then_inc(permT_kept, 1)
            pool.wait_ge(permT_kept, NB)
            for k in range(2):
                pool.tensor_copy(pg[:, k, :], permT[:, k, :]).then_inc(pg_ready, 1)
            with pool.Fori(1, NB // 2) as i:
                b = i * 2
                for k in range(2):
                    pool.wait_ge(c_done, b + (k - 1))
                    pool.tensor_copy(pg[:, k, :], permT[:, b + k, :]).then_inc(pg_ready, 1)

        @block.tensor
        def _(pe):
            def transpose_x(b, k):
                for h in range(KH):
                    last = pe.transpose(BX[:, h * P:(h + 1) * P], xn[:, k, h * P:(h + 1) * P], ident)
                last.then_inc(xT_done, 1)

            def project(dst, weight, src, done):
                for o in range(KH):
                    for i in range(KH):
                        last = pe.matmul(dst[:, o * P:(o + 1) * P], weight[:, i, o * P:(o + 1) * P],
                                         src[:, i, :], start=(i == 0), stop=(i == KH - 1))
                last.then_inc(done, 1)

            def project_v(k):
                for i in range(KH):
                    last = pe.matmul(BK[:, 0:E], cT[:, k, i, :], wv[:, i, :], start=(i == 0), stop=(i == KH - 1))
                last.then_inc(v_done, 1)

            def scores(k, c):
                pe.matmul(BS[c % 2][:, :], identb, causal, start=True, stop=False)
                pe.matmul(BS[c % 2][:, :], qz[:, k, c // 2, c % 2, :],
                          kd[:, k, c // 2].rearrange("p j t -> p (j t)"), start=False, stop=True).then_inc(s_done, 1)

            def transpose_p(c):
                for j in range(HC):
                    last = pe.transpose(BT[:, j * P:(j + 1) * P], pr[:, c % 2, j, :], ident)
                last.then_inc(pT_done, 1)

            def weigh_v(k, c):
                for j in range(HC):
                    last = pe.matmul(BO[j * DP:(j + 1) * DP, c * P:(c + 1) * P], va[:, k, c * HC + j, :],
                                     pT[:, c % 2, j * P:(j + 1) * P], start=True, stop=True,
                                     tile_position=(0, j * DP))
                last.then_inc(av_done, 1)

            def transpose_o():
                for c in range(NC):
                    last = pe.transpose(BX[:, c * P:(c + 1) * P], oT[:, c * P:(c + 1) * P], ident)
                last.then_inc(o_done, 1)

            def transpose_on():
                for h in range(KH):
                    last = pe.transpose(BQ[:, h * P:(h + 1) * P], on[:, h * P:(h + 1) * P], ident)
                last.then_inc(onT_done, 1)

            def project_o():
                for h in range(KH):
                    last = pe.matmul(BY[:, 0:E], onT[:, h, :], wo[:, h, :], start=(h == 0), stop=(h == KH - 1))
                last.then_inc(y_done, 1)

            def attend(b, k, ctx_count, first=False, second=False, final=False):
                for c in range(NC):
                    n = b * NC + c
                    if c == 0:
                        pe.wait_ge(q_ready, b + 1)
                        pe.wait_ge(k_ready, b + 1)
                    if not first or c >= 2:
                        pe.wait_ge(p_ready, n - 1)
                    scores(k, c)
                    if c == 3 and not first:
                        pe.wait_ge(on_ready, b)
                        if not final:
                            pe.wait_ge(q_ready, b + 2)
                        transpose_on()
                    if not first or c >= 2:
                        pe.wait_ge(pT_ready, n - 1)
                        if c == 2:
                            pe.wait_ge(v_ready, b + 1)
                            if not first:
                                pe.wait_ge(oT_ready, b)
                        weigh_v(k if c >= 2 else 1 - k, (c - 2) % NC)
                    if not first or c >= 1:
                        pe.wait_ge(p_ready, n)
                        if not first or c >= 2:
                            pe.wait_ge(pT_ready, n - 1)
                        transpose_p((c - 1) % NC)
                    if c == 0 and not final:
                        pe.wait_ge(xn_ready, b + 2)
                        if not first and not second:
                            pe.wait_ge(on_ready, b - 1)
                        transpose_x(b, 0)
                        pe.wait_ge(ctx_loaded[1 - k], ctx_count)
                        pe.wait_ge(v_ready, b + 1)
                        project(BK, wk, cT[:, 1 - k], k_done)
                    if c == 1 and not final:
                        pe.wait_ge(xT_ready, b + 2)
                        if not first and not second:
                            pe.wait_ge(onT_ready, b - 1)
                        project(BQ, wq, xT, q_done)
                    if c == 2:
                        if not final:
                            pe.wait_ge(k_ready, b + 2)
                            project_v(1 - k)
                        if not first:
                            pe.wait_ge(oT_ready, b)
                            transpose_o()
                    if c == 3 and not first:
                        pe.wait_ge(onT_ready, b)
                        if not second:
                            pe.wait_ge(x1_ready, b - 1)
                        project_o()

            pe.wait_ge(w_loaded[0], 16)
            pe.wait_ge(ctx_loaded[0], 16)
            project(BK, wk, cT[:, 0], k_done)
            pe.wait_ge(consts_loaded, 16)
            pe.wait_ge(xn_ready, 1)
            transpose_x(0, 0)
            pe.wait_ge(w_loaded[1], 16)
            pe.wait_ge(xT_ready, 1)
            project(BQ, wq, xT, q_done)
            pe.wait_ge(w_loaded[2], 16)
            pe.wait_ge(k_ready, 1)
            project_v(0)
            pe.wait_ge(w_loaded[3], 16)
            pe.wait_ge(maskb_ready, 1 + HC)
            attend(0, 0, 16, first=True)
            attend(1, 1, 32, second=True)
            attend(2, 0, 32)
            with pe.Fori(1, (NB - 1) // 2) as i:
                b = i * 2 + 1
                attend(b, 1, b * 8 + 24)
                attend(b + 1, 0, b * 8 + 24)
            attend(NB - 1, 1, 0, final=True)
            pe.wait_ge(pT_ready, NB * NC - 1)
            weigh_v(1, 2)
            pe.wait_ge(p_ready, NB * NC)
            transpose_p(3)
            pe.wait_ge(pT_ready, NB * NC)
            weigh_v(1, 3)
            pe.wait_ge(oT_ready, NB)
            transpose_o()
            pe.wait_ge(on_ready, NB)
            transpose_on()
            pe.wait_ge(onT_ready, NB)
            pe.wait_ge(x1_ready, NB - 1)
            project_o()

            BR, BL, BP = bank[0], bank[1], bank[2]
            BD = ((bank[3], bank[4]), (bank[5], bank[6]))

            def transpose_r(k4):
                for h in range(KH):
                    last = pe.transpose(BR[:, h * P:(h + 1) * P], xn[:, k4, h * P:(h + 1) * P], ident)
                last.then_inc(rT_done, 1)

            def logits():
                for h in range(KH):
                    last = pe.matmul(BL[:, 0:P], ctrl_sb[:, h, :], xT[:, h, :], start=(h == 0), stop=(h == KH - 1))
                last.then_inc(lg_done, 1)

            def route(b, k4, first=False, early=False, left=NB):
                k = k4 % 2
                pe.wait_ge(perm_ready, b + 1)
                if not first:
                    pe.wait_ge(pm_ready, b)
                pe.transpose(BP[:, 0:P], pc[:, k, :], ident).then_inc(pm_done, 1)
                if left > 1:
                    pe.wait_ge(rT_ready, b + 2)
                    pe.wait_ge(lt_ready, b + 1)
                    logits()
                if left > 2:
                    pe.wait_ge(rn_ready, b + 3)
                    transpose_r((k4 + 2) % 4)
                pe.wait_ge(pm_ready, b + 1)
                for h in range(KH):
                    if not early:
                        pe.wait_ge((d_kept0, d_kept1)[h], b - 1)
                    last = pe.matmul(BD[k][h][:, :], xn[:, k4, h * P:(h + 1) * P],
                                     permb[:, :, :].rearrange("p g s -> p (g s)"), start=True, stop=True)
                    last.then_inc((d_done0, d_done1)[h], 1)

            pe.wait_ge(small_loaded, 32)
            pe.wait_ge(rn_ready, 1)
            pe.wait_ge(x1_ready, NB)
            transpose_r(0)
            pe.wait_ge(rT_ready, 1)
            logits()
            pe.wait_ge(rn_ready, 2)
            transpose_r(1)
            for b in range(4):
                route(b, b, first=(b == 0), early=(b < 2))
            with pe.Fori(1, (NB - 4) // 4) as i:
                b = i * 4
                for k4 in range(4):
                    route(b + k4, k4)
            for k4 in range(4):
                route(NB - 4 + k4, k4, left=4 - k4)

            BH, BE = bank[0:2], bank[2:4]

            def expert_in(k4):
                k = k4 % 2
                for s in range(NS):
                    for h in range(KH):
                        last = pe.matmul(BH[k][s * F:(s + 1) * F, 0:GROUPS],
                                         wx[:, k4, h * P + s * F:h * P + (s + 1) * F], xe[:, k, h, s, :],
                                         start=(h == 0), stop=(h == KH - 1), tile_position=(0, s * F))
                last.then_inc(h_done, 1)

            def expert_out(k4):
                k = k4 % 2
                for h in range(KH):
                    last = pe.matmul(BE[k][:, h * E:(h + 1) * E], wx[:, k4, KH * P + h * P:KH * P + (h + 1) * P],
                                     hb[:, k].rearrange("p s g -> p (s g)"), start=True, stop=True)
                last.then_inc(e_done, 1)

            def expert(e, k4, loads, first=False, final=False):
                if not final:
                    pe.wait_ge(wx_loaded[(k4 + 1) % 4], loads)
                    pe.wait_ge(xe_ready, e + 2)
                    if not first:
                        pe.wait_ge(h_ready, e)
                    expert_in((k4 + 1) % 4)
                pe.wait_ge(h_ready, e + 1)
                if not isinstance(e, int) or e >= 2:
                    pe.wait_ge(e_kept, e - 1)
                expert_out(k4)

            pe.wait_ge(d_kept0, NB)
            pe.wait_ge(d_kept1, NB)
            pe.wait_ge(wx_loaded[0], 16)
            pe.wait_ge(xe_ready, 1)
            expert_in(0)
            for e in range(4):
                expert(e, e, 16 if e < 3 else 32, first=(e == 0))
            with pe.Fori(1, (NE - 4) // 4) as i:
                e = i * 4
                for k4 in range(4):
                    expert(e + k4, k4, e * 4 + (16 if k4 < 3 else 32))
            for k4 in range(4):
                expert(NE - 4 + k4, k4, 16 * (NE // 4), final=(k4 == 3))

            BY2, BC = (bank[4:6], bank[6:8]), bank[0:2]

            def transpose_y(k):
                for g in range(NG):
                    for h in range(KH):
                        o = (g % 2) * E + h * P
                        last = pe.transpose(BY2[k][g // 2][:, o:o + P], yg[:, k, h, g, :], ident)
                last.then_inc(yT_done, 1)

            def combine(b, k, early=False, final=False):
                if not final:
                    pe.wait_ge(yg_ready, b + 2)
                    if not isinstance(b, int) or b >= 1:
                        pe.wait_ge(ys_ready, b)
                    transpose_y(1 - k)
                pe.wait_ge(ys_ready, b + 1)
                pe.wait_ge(pg_ready, b + 1)
                if not early:
                    pe.wait_ge(yo_ready, b - 1)
                for g in range(NG):
                    last = pe.matmul(BC[k][g * T:(g + 1) * T, 0:E], pg[:, k, g * T:(g + 1) * T],
                                     ys[:, k, g, :], start=True, stop=True, tile_position=(0, g * T))
                last.then_inc(c_done, 1)

            pe.wait_ge(e_kept, NE)
            pe.wait_ge(yg_ready, 1)
            transpose_y(0)
            combine(0, 0, early=True)
            combine(1, 1, early=True)
            with pe.Fori(1, (NB - 2) // 2) as i:
                b = i * 2
                for k in range(2):
                    combine(b + k, k)
            combine(NB - 2, 0)
            combine(NB - 1, 1, final=True)

        @block.scalar
        def _(act):
            for i in range(4):
                act.dma_start(w[:, i], wattn[:, i]).then_inc(w_loaded[i], 16)
            act.dma_start(cf[:, :], constf).then_inc(consts_loaded, 16)
            act.dma_start(gates_sb[:, :], gates).then_inc(gates_loaded, 16)
            act.dma_start(bo_sb[:, :], bo).then_inc(gates_loaded, 16)
            act.wait_ge(gates_loaded, 32)
            act.activation(tg[:, :], gates_sb[:, :], ACT.Tanh).then_inc(tanh_ready, 1)
            act.wait_ge(var_ready, 1)
            act.activation(sd[:, :], ve[:, :], ACT.Sqrt).then_inc(sd_ready, 1)

            def keep_x():
                act.activation(xT[:, :, :], BX[:, 0:E].rearrange("p (h t) -> p h t", h=KH), ACT.Copy)\
                    .then_inc(xT_ready, 1)

            def keep_q(k):
                for r in range(2):
                    last = act.activation(qz[64 * r:64 * r + 64, k, :, r, :],
                                          BQ[64 * r:64 * r + 64, 0:E].rearrange("p (h t) -> p h t", h=KH),
                                          ACT.Copy, scale=float(D) ** -0.5)
                last.then_inc(q_ready, 1)

            def keep_v(k):
                act.activation(va[:, k, :, 0:D], BK[:, 0:E].rearrange("p (h d) -> p h d", h=H), ACT.Copy)\
                    .then_inc(v_ready, 1)

            def keep_oT():
                act.activation(oT[:, :], BO[:, :], ACT.Copy).then_inc(oT_ready, 1)

            def keep_onT():
                act.activation(onT[:, :, :], BQ[:, 0:E].rearrange("p (h t) -> p h t", h=KH), ACT.Copy)\
                    .then_inc(onT_ready, 1)

            def softmax(b, k, first=False, final=False):
                for c in range(NC):
                    n = b * NC + c
                    if c == 1 and not first:
                        act.wait_ge(av_done, b * NC)
                        keep_oT()
                    if c == 3 and not first:
                        act.wait_ge(onT_done, b)
                        keep_onT()
                    act.wait_ge(max_ready, n + 1)
                    if not first or c >= 2:
                        act.wait_ge(pT_done, n - 1)
                    for j in range(HC):
                        last = act.activation(pr[:, c % 2, j, :], BS[c % 2][:, j * P:(j + 1) * P], ACT.Exp,
                                              bias=nmax[:, c * HC + j:c * HC + j + 1])
                    last.then_inc(p_ready, 1)
                    if c == 0 and not final:
                        act.wait_ge(xT_done, b + 2)
                        keep_x()
                    if c == 1 and not final:
                        act.wait_ge(q_done, b + 2)
                        keep_q(1 - k)
                    if c == 2 and not final:
                        act.wait_ge(v_done, b + 2)
                        keep_v(1 - k)

            act.wait_ge(xT_done, 1)
            keep_x()
            act.wait_ge(q_done, 1)
            act.wait_ge(zeroed, 2)
            keep_q(0)
            act.wait_ge(v_done, 1)
            keep_v(0)
            softmax(0, 0, first=True)
            with act.Fori(0, (NB - 1) // 2) as i:
                b = i * 2 + 1
                for k in range(2):
                    softmax(b + k, 1 - k)
            softmax(NB - 1, 1, final=True)
            act.wait_ge(av_done, NB * NC)
            keep_oT()
            act.wait_ge(onT_done, NB)
            keep_onT()
            act.wait_ge(var_ready, 2)
            act.activation(sd[:, :], ve[:, :], ACT.Sqrt).then_inc(sd_ready, 1)

            def keep_r():
                act.activation(xT[:, :, :], bank[0][:, 0:E].rearrange("p (h t) -> p h t", h=KH), ACT.Copy)\
                    .then_inc(rT_ready, 1)

            def keep_d(b, k):
                act.wait_ge(d_done0, b + 1)
                act.activation(routed[:, 0, bass.ds(b * NG, NG), :],
                               bank[3 + 2 * k][:, :].rearrange("p (g s) -> p g s", g=NG), ACT.Copy)\
                    .then_inc(d_kept0, 1)

            for b in range(2):
                act.wait_ge(rT_done, b + 1)
                keep_r()
            with act.Fori(0, (NB - 2) // 2) as i:
                b = i * 2
                for k in range(2):
                    act.wait_ge(rT_done, b + (k + 3))
                    keep_r()
                    keep_d(b + k, k)
            for k in range(2):
                keep_d(NB - 2 + k, k)

            with act.Fori(0, NE // 2) as i:
                e = i * 2
                for k in range(2):
                    act.wait_ge(e_done, e + (k + 1))
                    act.activation(routed[:, :, :, bass.ds((e + k) * NS, NS)],
                                   bank[2 + k][:, :].rearrange("p (h s g) -> p h g s", h=KH, s=NS), ACT.Copy)\
                        .then_inc(e_kept, 1)

            with act.Fori(0, NB // 2) as i:
                b = i * 2
                for k in range(2):
                    act.wait_ge(yT_done, b + (k + 1))
                    for q in range(2):
                        last = act.activation(ys[:, k, 2 * q:2 * q + 2, :],
                                              bank[4 + 2 * k + q][:, :].rearrange("p (g e) -> p g e", g=2), ACT.Copy)
                    last.then_inc(ys_ready, 1)

        @block.vector
        def _(dve):
            def rstd(step):
                n = 5 * step
                dve.wait_ge(sd_ready, step + 1)
                dve.reciprocal(rs[:, :], sd[:, :]).then_inc(rs_step, 1)
                dve.wait_ge(rs_step, n + 1)
                dve.tensor_tensor(nt[:, :], ve[:, :], rs[:, :], ALU.mult).then_inc(rs_step, 1)
                dve.wait_ge(rs_step, n + 2)
                dve.tensor_tensor(nt[:, :], nt[:, :], rs[:, :], ALU.mult).then_inc(rs_step, 1)
                dve.wait_ge(rs_step, n + 3)
                dve.tensor_scalar(nt[:, :], nt[:, :], -0.5, 1.5, ALU.mult, ALU.add).then_inc(rs_step, 1)
                dve.wait_ge(rs_step, n + 4)
                dve.tensor_tensor(rs[:, :], rs[:, :], nt[:, :], ALU.mult).then_inc(rs_step, 1)
                dve.wait_ge(rs_step, n + 5)

            def moments(step):
                n = 4 * step
                mean, half = mv[:, :, 0], mv[:, :, 1]
                dve.tensor_tensor(mean, stats[:, :, 1], stats[:, :, 4], ALU.add).then_inc(mom_step, 1)
                dve.tensor_tensor(half, stats[:, :, 1], stats[:, :, 4], ALU.subtract).then_inc(mom_step, 1)
                dve.tensor_tensor(ve[:, :], stats[:, :, 2], stats[:, :, 5], ALU.add).then_inc(mom_step, 1)
                dve.wait_ge(mom_step, n + 3)
                dve.tensor_scalar(mean, mean, 0.5, None, ALU.mult)
                dve.tensor_tensor(half, half, half, ALU.mult)
                dve.tensor_scalar(ve[:, :], ve[:, :], 1.0 / E, EPS, ALU.mult, ALU.add).then_inc(mom_step, 1)
                dve.wait_ge(mom_step, n + 4)
                dve.scalar_tensor_tensor(ve[:, :], half, 0.25, ve[:, :], ALU.mult, ALU.add).then_inc(var_ready, 1)

            for i in range(NB // XC):
                dve.wait_ge(x_loaded[i], 16)
                for b in range(i * XC, (i + 1) * XC):
                    last = dve.bn_stats(stats[:, b, :], xs[:, b, :])
            last.then_inc(stats_ready, 1)
            dve.wait_ge(stats_ready, 1)
            moments(0)
            dve.wait_ge(gates_loaded, 32)
            dve.wait_ge(tanh_ready, 1)
            dve.tensor_scalar(bo_sb[:, :], bo_sb[:, :], tg[:, 0:1], None, ALU.mult).then_inc(bo_ready, 1)
            rstd(0)

            def normalize(b, k, ready):
                dve.tensor_scalar(xn[:, k, :], xs[:, b, :], mv[:, b, 0:1], rs[:, bass.ds(b, 1)],
                                  ALU.subtract, ALU.mult).then_inc(ready, 1)

            def keep_k(k):
                for h in range(KH):
                    last = dve.tensor_tensor(kd[:, k, h], BK[:, None, h * P:(h + 1) * P].to_broadcast([P, HC, P]),
                                             headmask[:, :, None].to_broadcast([P, HC, P]), ALU.mult)
                last.then_inc(k_ready, 1)

            def normalize_o(count):
                o = BX[:, :].rearrange("p (h r) -> p h r", h=H)
                dve.reciprocal(rsum[:, :], o[:, :, D]).then_inc(rsum_ready, 1)
                dve.wait_ge(rsum_ready, count)
                dve.tensor_tensor(on[:, :].rearrange("p (h d) -> p h d", h=H), o[:, :, 0:D],
                                  rsum[:, :, None].to_broadcast([P, H, D]), ALU.mult).then_inc(on_ready, 1)

            def residual(b):
                dve.scalar_tensor_tensor(xs[:, b, :], BY[:, 0:E], tg[:, 0:1], xs[:, b, :], ALU.mult, ALU.add)\
                    .then_inc(x1_ready, 1)

            def attend(b, k, first=False, second=False, last_but_one=False, final=False):
                for c in range(NC):
                    n = b * NC + c
                    dve.wait_ge(s_done, n + 1)
                    dve.tensor_reduce(nmax[:, c * HC:(c + 1) * HC], BS[c % 2][:, :].rearrange("p (j t) -> p j t", j=HC),
                                      AX_X, ALU.max, negate=True).then_inc(max_ready, 1)
                    if c == 3 and not first:
                        dve.wait_ge(o_done, b)
                        normalize_o(b)
                    if not first or c >= 1:
                        dve.wait_ge(pT_done, n)
                        dve.tensor_copy(pT[:, (c - 1) % 2, :], BT[:, :]).then_inc(pT_ready, 1)
                    if c == 0 and not final:
                        dve.wait_ge(k_done, b + 2)
                        keep_k(1 - k)
                    if c == 0 and not first and not second:
                        dve.wait_ge(y_done, b - 1)
                        dve.wait_ge(xb_ready, b - 1)
                        residual(b - 2)
                    if c == 1 and not first and not second:
                        dve.wait_ge(x1_ready, b - 1)
                        dve.bn_stats(stats[:, b - 2, :], xs[:, b - 2, :])
                    if c == 3 and not final and not last_but_one:
                        dve.wait_ge(xT_done, b + 2)
                        normalize(b + 2, 0, xn_ready)

            normalize(0, 0, xn_ready)
            dve.wait_ge(consts_loaded, 16)
            dve.wait_ge(k_done, 1)
            keep_k(0)
            dve.wait_ge(xT_done, 1)
            normalize(1, 0, xn_ready)
            attend(0, 0, first=True)
            attend(1, 1, second=True)
            with dve.Fori(1, (NB - 2) // 2) as i:
                b = i * 2
                for k in range(2):
                    attend(b + k, k)
            attend(NB - 2, 0, last_but_one=True)
            attend(NB - 1, 1, final=True)
            dve.wait_ge(pT_done, NB * NC)
            dve.tensor_copy(pT[:, 1, :], BT[:, :]).then_inc(pT_ready, 1)
            for b in (NB - 2, NB - 1):
                if b == NB - 1:
                    dve.wait_ge(o_done, NB)
                    normalize_o(NB)
                dve.wait_ge(y_done, b + 1)
                dve.wait_ge(xb_ready, b + 1)
                residual(b)
                dve.wait_ge(x1_ready, b + 1)
                last = dve.bn_stats(stats[:, b, :], xs[:, b, :])
            last.then_inc(stats_ready, 1)
            dve.wait_ge(stats_ready, 2)
            moments(1)
            rstd(1)

            def choose(b, k, early):
                dve.wait_ge(lg_done, b + 1)
                dve.tensor_tensor(lt[:, :], bank[1][:, 0:P], tie, ALU.add).then_inc(lt_ready, 1)
                dve.wait_ge(lt_ready, b + 1)
                lg = lt[:, :].rearrange("p (g t) -> p g t", g=NG)
                dve.tensor_reduce(gmax[:, :], lg, AX_X, ALU.max).then_inc(gmax_ready, 1)
                dve.wait_ge(gmax_ready, b + 1)
                if not early:
                    dve.wait_ge(permT_kept, b - 1)
                dve.tensor_tensor(pc[:, k, :].rearrange("p (g t) -> p g t", g=NG), lg,
                                  gmax[:, :, None].to_broadcast([P, NG, T]), ALU.is_equal).then_inc(perm_ready, 1)

            def spread(b):
                dve.wait_ge(pm_done, b + 1)
                dve.tensor_tensor(permb[:, :, :], bank[2][:, None, 0:P].to_broadcast([P, NG, P]),
                                  groupmask[:, :, None].to_broadcast([P, NG, P]), ALU.mult).then_inc(pm_ready, 1)

            def keep_d(b, k):
                dve.wait_ge(d_done1, b + 1)
                dve.tensor_copy(routed[:, 1, bass.ds(b * NG, NG), :],
                                bank[4 + 2 * k][:, :].rearrange("p (g s) -> p g s", g=NG)).then_inc(d_kept1, 1)

            def route(b, k4, left=NB):
                spread(b)
                if left > 1:
                    choose(b + 1, (k4 + 1) % 2, isinstance(b, int) and b == 0)
                if left > 3:
                    normalize(b + 3, (k4 + 3) % 4, rn_ready)
                keep_d(b, k4 % 2)

            for b in range(3):
                normalize(b, b, rn_ready)
            choose(0, 0, True)
            for b in range(4):
                route(b, b)
            with dve.Fori(1, (NB - 4) // 4) as i:
                b = i * 4
                for k4 in range(4):
                    route(b + k4, k4)
            for k4 in range(4):
                route(NB - 4 + k4, k4, left=4 - k4)

            def stage(e, k):
                dve.tensor_copy(xe[:, k].rearrange("p h s g -> p h g s"),
                                routed[:, :, :, bass.ds(e * NS, NS)]).then_inc(xe_ready, 1)

            def hidden(e, k):
                for s in range(NS):
                    r = slice(s * F, (s + 1) * F)
                    last = dve.tensor_scalar(hb[r, k, s, :], bank[k][r, 0:GROUPS], ebias_sb[r, bass.ds(e, 1)], 0.0,
                                             ALU.add, ALU.max)
                last.then_inc(h_ready, 1)

            dve.wait_ge(d_kept0, NB)
            dve.wait_ge(d_kept1, NB)
            stage(0, 0)
            stage(1, 1)
            dve.wait_ge(zeroed, 3)
            for e in range(2):
                dve.wait_ge(h_done, e + 1)
                hidden(e, e)
                stage(e + 2, e)
            with dve.Fori(1, (NE - 2) // 2) as i:
                e = i * 2
                for k in range(2):
                    dve.wait_ge(h_done, e + (k + 1))
                    dve.wait_ge(e_done, e + (k - 1))
                    hidden(e + k, k)
                    stage(e + (k + 2), k)
            for k in range(2):
                dve.wait_ge(h_done, NE - 1 + k)
                dve.wait_ge(e_done, NE - 3 + k)
                hidden(NE - 2 + k, k)

            def stage_y(b, k):
                dve.tensor_copy(yg[:, k], routed[:, :, bass.ds(b * NG, NG), :]).then_inc(yg_ready, 1)

            def finish(b, k):
                dve.wait_ge(c_done, b + 1)
                dve.scalar_tensor_tensor(yo[:, k, :], bank[k][:, 0:E], tg[:, 1:2], xs[:, b, :], ALU.mult, ALU.add)\
                    .then_inc(yo_ready, 1)

            dve.wait_ge(e_kept, NE)
            stage_y(0, 0)
            stage_y(1, 1)
            for k in range(2):
                dve.wait_ge(yT_done, k + 1)
                stage_y(k + 2, k)
                finish(k, k)
            with dve.Fori(1, (NB - 2) // 2) as i:
                b = i * 2
                for k in range(2):
                    dve.wait_ge(yT_done, b + (k + 1))
                    stage_y(b + (k + 2), k)
                    dve.wait_ge(stored[k], b * 8)
                    finish(b + k, k)
            for k in range(2):
                dve.wait_ge(stored[k], 8 * (NB - 2))
                finish(NB - 2 + k, k)


def constants():
    import numpy as np

    rows = np.arange(P)
    ident = np.eye(P, dtype=np.float32)
    heads = ((rows[:, None] // D) % HC == np.arange(HC)[None, :]).astype(np.float32)
    step = np.arange(T, dtype=np.float32) * (np.float32(1e-6) / np.float32(T - 1))
    ramp = np.broadcast_to(np.tile(step, NG)[None, :], (P, P))
    groups = (rows[:, None] // T == np.arange(NG)[None, :]).astype(np.float32)
    mask = np.where(rows[None, :] <= rows[:, None], 0.0, NEG).astype(np.float32)
    return np.concatenate([ident, heads, ramp, groups, mask], axis=1)


def kernel(**inputs):
    import numpy as _np
    import concourse.bacc as _bacc
    from concourse import mybir as _mybir
    from concourse.bass_utils import run_bass_kernel_spmd as _run

    a = {name: _np.asarray(v) for name, v in inputs.items()}

    def halves(m):
        return m.reshape(KH, P, -1).transpose(1, 0, 2)

    f1 = a["L0_ffn_f1"].reshape(KH, P, NE, NS * F).transpose(2, 1, 0, 3).reshape(NE, P, KH * NS * F)
    f2 = a["L0_ffn_f2"].reshape(NE, NS * F, E)
    laid = {
        "x": a["x"],
        "ctxT": a["ctx_1024"].reshape(NB, P, KH, P).transpose(0, 3, 2, 1),
        "wattn": _np.stack([halves(a["L0_xattn_" + n].T) for n in ("Wk", "Wq", "Wv", "Wo")], axis=1),
        "bo": _np.broadcast_to(a["L0_xattn_bo"], (P, E)),
        "gates": _np.broadcast_to(_np.concatenate([a["g_xattn"], a["g_ffn"]]), (P, 2)),
        "ctrl": halves(a["L0_ffn_controller"].reshape(E, SLOTS)),
        "wexp": _np.concatenate([f1, f2], axis=2),
        "ebias": a["L0_ffn_bias"].reshape(NE, NS * F).T,
        "constf": constants(),
    }
    nc = _bacc.Bacc("TRN2", target_bir_lowering=False, num_devices=1)
    arrays, args = {}, []
    for name, v in laid.items():
        v = _np.ascontiguousarray(v)
        arrays[f"in_{name}_dram"] = v
        args.append(nc.dram_tensor(f"in_{name}_dram", v.shape, _mybir.dt.from_np(v.dtype), kind="ExternalInput").ap())
    args.append(nc.dram_tensor("out_0_dram", (NB, P, E), F32, kind="ExternalOutput").ap())
    build(nc, *args)
    r = _run(nc, [arrays], core_ids=[0])
    return r.results[0]["out_0_dram"]
```

```python
from contextlib import ExitStack

import concourse.bass as bass
from concourse import mybir

F32 = mybir.dt.float32
F32R = mybir.dt.float32r
BF16 = mybir.dt.bfloat16
ALU = mybir.AluOpType
ACT = mybir.ActivationFunctionType
AX_X = mybir.AxisListType.X

P = 128
NB = 16
E = 256
KH = E // P
H = 16
D = E // H
HC = 4
NC = H // HC
DP = 32
NE, NS, F = 32, 4, 32
SLOTS = NE * NS
T = 32
NG = P // T
GROUPS = NB * NG
RING = 4
XC = 4
EPS = 1e-5
NEG = -(2.0 ** 100)


def build(nc, x, ctxT, wattn, bo, gates, ctrl, wexp, ebias, constf, out):
    with ExitStack() as ctx:
        def sb(name, shape, dt=F32):
            return ctx.enter_context(nc.sbuf_tensor(name, shape, dt))

        def sem(name):
            return ctx.enter_context(nc.semaphore(name))

        bank = [ctx.enter_context(nc.psum_tensor(f"bank{i}", [P, 512], F32)) for i in range(8)]

        cf = sb("cf", [P, P + HC + P + NG + DP])
        ident = cf[:, 0:P]
        headmask = cf[:, P:P + HC]
        tie = cf[:, P + HC:P + HC + P]
        groupmask = cf[:, P + HC + P:P + HC + P + NG]
        mask = cf[:, P + HC + P + NG:P + HC + P + NG + DP]
        cb = sb("cb", [P, P + HC * DP], BF16)
        identb = cb[:, 0:P]
        causal = cb[:, P:P + HC * DP]
        w = sb("w", [P, 4, KH, E])
        wh = sb("wh", [P, 2, KH, E], F32R)
        wl = sb("wl", [P, 2, KH, E], F32R)
        wk, wq, WV, WO = w[:, 0], w[:, 1], 0, 1
        bo_sb = sb("bo_sb", [P, E])
        gates_sb = sb("gates_sb", [P, 2])
        tg = sb("tg", [P, 2])
        ctrl_sb = sb("ctrl_sb", [P, KH, SLOTS])
        ebias_sb = sb("ebias_sb", [P, NE])

        xs = sb("xs", [P, NB, E])
        stats = sb("stats", [P, NB, 6])
        mv = sb("mv", [P, NB, 2])
        ve = sb("ve", [P, NB])
        sd = sb("sd", [P, NB])
        rs = sb("rs", [P, NB])
        nt = sb("nt", [P, NB])
        xn = sb("xn", [P, 4, E])
        xT = sb("xT", [P, KH, P])
        cTh = sb("cTh", [P, 2, KH, P], F32R)
        cTl = sb("cTl", [P, 2, KH, P], F32R)
        cT = sb("cT", [P, 2, KH, P])
        kd = sb("kd", [P, 2, KH, HC, P])
        qz = sb("qz", [P, 2, KH, 2, P])
        va = sb("va", [P, 2, H, DP])
        nmax = sb("nmax", [P, H])
        pr = sb("pr", [P, 2, HC, P])
        pT = sb("pT", [P, 2, HC * P])
        oT = sb("oT", [P, NC * P])
        rsum = sb("rsum", [P, H])
        on = sb("on", [P, E])
        onTh = sb("onTh", [P, KH, P], F32R)
        onTl = sb("onTl", [P, KH, P], F32R)

        rT = sb("rT", [P, KH, P])
        rh = sb("rh", [P, 4, E], F32R)
        rl = sb("rl", [P, 4, E], F32R)
        lt = sb("lt", [P, P])
        gmax = sb("gmax", [P, NG])
        pc = sb("pc", [P, 2, P])
        permT = sb("permT", [P, NB, P])
        permb = sb("permb", [P, NG, P], F32R)
        routed = sb("routed", [P, KH, GROUPS, SLOTS])
        wx = sb("wx", [P, RING, KH * P + E])
        xe = sb("xe", [P, 2, KH, NS, GROUPS])
        hb = sb("hb", [P, 2, NS, GROUPS])
        yg = sb("yg", [P, 2, KH, NG, SLOTS])
        pg = sb("pg", [P, 2, P])
        ys = sb("ys", [P, 2, NG, E])
        yo = sb("yo", [P, 2, E])

        x_loaded = [sem(f"x_loaded{i}") for i in range(NB // XC)]
        consts_loaded = sem("consts_loaded")
        maskb_ready = sem("maskb_ready")
        small_loaded = sem("small_loaded")
        gates_loaded = sem("gates_loaded")
        w_loaded = [sem(f"w_loaded{i}") for i in range(4)]
        ctx_loaded = [sem(f"ctx_loaded{i}") for i in range(2)]
        wx_loaded = [sem(f"wx_loaded{i}") for i in range(RING)]
        stored = [sem(f"stored{i}") for i in range(2)]
        zeroed = sem("zeroed")
        above_ready = sem("above_ready")
        w_high = sem("w_high")
        w_ready = sem("w_ready")
        stats_ready = sem("stats_ready")
        var_ready = sem("var_ready")
        sd_ready = sem("sd_ready")
        rs_step = sem("rs_step")
        mom_step = sem("mom_step")
        tanh_ready = sem("tanh_ready")
        bo_ready = sem("bo_ready")
        xn_ready = sem("xn_ready")
        xT_done = sem("xT_done")
        xT_ready = sem("xT_ready")
        c_high = sem("c_high")
        c_ready = sem("c_ready")
        k_done = sem("k_done")
        k_ready = sem("k_ready")
        q_done = sem("q_done")
        q_ready = sem("q_ready")
        v_done = sem("v_done")
        v_ready = sem("v_ready")
        oT_ready = sem("oT_ready")
        o_done = sem("o_done")
        rsum_ready = sem("rsum_ready")
        on_ready = sem("on_ready")
        onT_done = sem("onT_done")
        onTh_ready = sem("onTh_ready")
        onTl_ready = sem("onTl_ready")
        y_done = sem("y_done")
        xb_ready = sem("xb_ready")
        x1_ready = sem("x1_ready")
        s_done = sem("s_done")
        max_ready = sem("max_ready")
        p_ready = sem("p_ready")
        pT_done = sem("pT_done")
        pT_ready = sem("pT_ready")
        av_done = sem("av_done")
        rn_ready = sem("rn_ready")
        rh_ready = sem("rh_ready")
        rl_ready = sem("rl_ready")
        rT_done = sem("rT_done")
        rT_ready = sem("rT_ready")
        lg_done = sem("lg_done")
        lt_ready = sem("lt_ready")
        gmax_ready = sem("gmax_ready")
        perm_ready = sem("perm_ready")
        pm_done = sem("pm_done")
        pm_ready = sem("pm_ready")
        d_done = sem("d_done")
        d_kept = sem("d_kept")
        xe_ready = sem("xe_ready")
        h_done = sem("h_done")
        h_ready = sem("h_ready")
        e_done = sem("e_done")
        e_kept = sem("e_kept")
        permT_kept = sem("permT_kept")
        yg_ready = sem("yg_ready")
        pg_ready = sem("pg_ready")
        yT_done = sem("yT_done")
        ys_ready = sem("ys_ready")
        c_done = sem("c_done")
        yo_ready = sem("yo_ready")

        BS, BT, BO, BX, BK, BQ, BY = bank[0:2], bank[2], bank[3], bank[4], bank[5], bank[6], bank[7]

        block = ctx.enter_context(nc.Block())

        @block.sync
        def _(sp):
            sp.dma_start(xs[:, 0:XC, :], x[0:XC].rearrange("b s e -> s b e")).then_inc(x_loaded[0], 16)
            sp.dma_start(cT[:, 0], ctxT[0]).then_inc(ctx_loaded[0], 16)
            for i in range(1, NB // XC):
                sp.dma_start(xs[:, i * XC:(i + 1) * XC, :],
                             x[i * XC:(i + 1) * XC].rearrange("b s e -> s b e")).then_inc(x_loaded[i], 16)
            sp.dma_start(cT[:, 1], ctxT[1]).then_inc(ctx_loaded[1], 16)
            sp.dma_start(ctrl_sb[:, :, :], ctrl).then_inc(small_loaded, 16)
            sp.dma_start(ebias_sb[:, :], ebias).then_inc(small_loaded, 16)
            for r in range(RING):
                sp.dma_start(wx[:, r], wexp[r]).then_inc(wx_loaded[r], 16)
            with sp.Fori(1, NB // 2) as i:
                b = i * 2
                for k in range(2):
                    sp.wait_ge(c_ready, b + (k - 1))
                    sp.wait_ge(k_done, b + (k - 1))
                    sp.dma_start(cT[:, k], ctxT[b + k]).then_inc(ctx_loaded[k], 16)
            with sp.Fori(1, NE // RING) as i:
                e = i * RING
                for r in range(RING):
                    sp.wait_ge(e_done, e + (r - RING + 1))
                    sp.dma_start(wx[:, r], wexp[e + r]).then_inc(wx_loaded[r], 16)
            with sp.Fori(0, NB // 2) as i:
                b = i * 2
                for k in range(2):
                    sp.wait_ge(yo_ready, b + (k + 1))
                    sp.dma_start(out[b + k], yo[:, k]).then_inc(stored[k], 16)
            for k in range(2):
                sp.wait_ge(stored[k], 16 * (NB // 2))


        @block.gpsimd
        def _(pool):
            pool.memset(qz[:, :, :, :, :], 0.0).then_inc(zeroed, 1)
            pool.memset(va[:, :, :, :], 1.0).then_inc(zeroed, 1)
            pool.memset(hb[:, :, :, :], 0.0).then_inc(zeroed, 1)
            pool.wait_ge(consts_loaded, 16)
            pool.tensor_copy(identb, ident).then_inc(maskb_ready, 1)
            for j in range(HC):
                pool.tensor_copy(causal[:, j * DP:(j + 1) * DP], mask).then_inc(maskb_ready, 1)

            def split_context(k, n):
                pool.wait_ge(c_high, n)
                pool.tensor_tensor(cTl[:, k], cT[:, k], cTh[:, k].bitcast(F32), ALU.subtract).then_inc(c_ready, 1)

            def bias_x(b):
                pool.wait_ge(xn_ready, b + 1)
                pool.tensor_tensor(xs[:, b, :], xs[:, b, :], bo_sb[:, :], ALU.add).then_inc(xb_ready, 1)

            for k in range(2):
                split_context(k, k + 1)
            pool.wait_ge(bo_ready, 1)
            for k in range(2):
                bias_x(k)
            with pool.Fori(1, NB // 2) as i:
                b = i * 2
                for k in range(2):
                    split_context(k, b + (k + 1))
                    bias_x(b + k)

            def split_rows(b, k4):
                pool.wait_ge(rh_ready, b + 1)
                pool.tensor_tensor(rl[:, k4], xn[:, k4], rh[:, k4].bitcast(F32), ALU.subtract).then_inc(rl_ready, 1)

            def keep_perm(b, k):
                pool.wait_ge(perm_ready, b + 1)
                pool.tensor_copy(permT[:, b, :], pc[:, k, :]).then_inc(permT_kept, 1)

            for b in range(2):
                split_rows(b, b)
            with pool.Fori(0, NB // 4 - 1) as i:
                b = i * 4
                for k4 in range(4):
                    split_rows(b + (k4 + 2), (k4 + 2) % 4)
                    keep_perm(b + k4, k4 % 2)
            for k4 in range(4):
                if k4 < 2:
                    split_rows(NB - 2 + k4, k4 + 2)
                keep_perm(NB - 4 + k4, k4 % 2)
            pool.wait_ge(permT_kept, NB)
            for k in range(2):
                pool.tensor_copy(pg[:, k, :], permT[:, k, :]).then_inc(pg_ready, 1)
            with pool.Fori(1, NB // 2) as i:
                b = i * 2
                for k in range(2):
                    pool.wait_ge(c_done, b + (k - 1))
                    pool.tensor_copy(pg[:, k, :], permT[:, b + k, :]).then_inc(pg_ready, 1)

        @block.tensor
        def _(pe):
            def transpose_x(b, k):
                for h in range(KH):
                    last = pe.transpose(BX[:, h * P:(h + 1) * P], xn[:, k, h * P:(h + 1) * P], ident)
                last.then_inc(xT_done, 1)

            def project(dst, weight, src, done):
                for o in range(KH):
                    for i in range(KH):
                        last = pe.matmul(dst[:, o * P:(o + 1) * P], weight[:, i, o * P:(o + 1) * P],
                                         src[:, i, :], start=(i == 0), stop=(i == KH - 1))
                last.then_inc(done, 1)

            def project_rows(dst, high, low, m, done):
                parts = [(src[:, i, :], wt[:, m, i, :])
                         for i in range(KH) for src, wt in ((high, wh), (low, wh), (high, wl))]
                for q, (stationary, moving) in enumerate(parts):
                    last = pe.matmul(dst[:, 0:E], stationary, moving, start=(q == 0), stop=(q == len(parts) - 1))
                last.then_inc(done, 1)

            def scores(k, c):
                bs = BS[c % 2][:, :].rearrange("p (h t) -> p h t", h=HC)
                for j in range(P // DP):
                    r = slice(j * DP, (j + 1) * DP)
                    pe.matmul(bs[r, :, r], identb[:, r], causal, start=True, stop=False,
                              tile_position=(0, j * DP), skip_group_check=True)
                for j in range(P // DP):
                    r = slice(j * DP, (j + 1) * DP)
                    last = pe.matmul(bs[r, :, 0:(j + 1) * DP], qz[:, k, c // 2, c % 2, r],
                                     kd[:, k, c // 2, :, 0:(j + 1) * DP], start=False, stop=True,
                                     tile_position=(0, j * DP), skip_group_check=True)
                last.then_inc(s_done, 1)

            def transpose_p(c):
                for j in range(HC):
                    last = pe.transpose(BT[:, j * P:(j + 1) * P], pr[:, c % 2, j, :], ident)
                last.then_inc(pT_done, 1)

            def weigh_v(k, c):
                for j in range(HC):
                    last = pe.matmul(BO[j * DP:(j + 1) * DP, c * P:(c + 1) * P], va[:, k, c * HC + j, :],
                                     pT[:, c % 2, j * P:(j + 1) * P], start=True, stop=True,
                                     tile_position=(0, j * DP))
                last.then_inc(av_done, 1)

            def transpose_o():
                for c in range(NC):
                    last = pe.transpose(BX[:, c * P:(c + 1) * P], oT[:, c * P:(c + 1) * P], ident)
                last.then_inc(o_done, 1)

            def transpose_on():
                for h in range(KH):
                    last = pe.transpose(BQ[:, h * P:(h + 1) * P], on[:, h * P:(h + 1) * P], ident)
                last.then_inc(onT_done, 1)

            def attend(b, k, first=False, second=False, third=False, final=False):
                for c in range(NC):
                    n = b * NC + c
                    if c == 0:
                        pe.wait_ge(q_ready, b + 1)
                        pe.wait_ge(k_ready, b + 1)
                    if not first or c >= 2:
                        pe.wait_ge(p_ready, n - 1)
                    scores(k, c)
                    if not first or c == 3:
                        pe.wait_ge(pT_ready, n - 2)
                        if c == 3:
                            pe.wait_ge(v_ready, b + 1)
                            if not first:
                                pe.wait_ge(oT_ready, b)
                        weigh_v(k if c == 3 else 1 - k, (c - 3) % NC)
                    if not first or c >= 2:
                        transpose_p((c - 2) % NC)
                    if c == 0 and not final:
                        pe.wait_ge(c_high, b + 2)
                        pe.wait_ge(v_ready, b + 1)
                        project(BK, wk, cT[:, 1 - k], k_done)
                    if c == 0 and not first and not second:
                        pe.wait_ge(on_ready, b - 1)
                        transpose_on()
                    if c == 1 and not final:
                        pe.wait_ge(xn_ready, b + 2)
                        transpose_x(b, 0)
                    if c == 1 and not first and not second:
                        pe.wait_ge(onTl_ready, b - 1)
                        if not third:
                            pe.wait_ge(x1_ready, b - 2)
                        project_rows(BY, onTh, onTl, WO, y_done)
                    if c == 2 and not final:
                        pe.wait_ge(xT_ready, b + 2)
                        project(BQ, wq, xT, q_done)
                    if c == 3:
                        if not final:
                            pe.wait_ge(k_ready, b + 2)
                            pe.wait_ge(c_ready, b + 2)
                            project_rows(BK, cTh[:, 1 - k], cTl[:, 1 - k], WV, v_done)
                        if not first:
                            pe.wait_ge(oT_ready, b)
                            transpose_o()

            pe.wait_ge(w_loaded[0], 16)
            pe.wait_ge(c_high, 1)
            project(BK, wk, cT[:, 0], k_done)
            pe.wait_ge(consts_loaded, 16)
            pe.wait_ge(xn_ready, 1)
            transpose_x(0, 0)
            pe.wait_ge(w_loaded[1], 16)
            pe.wait_ge(xT_ready, 1)
            project(BQ, wq, xT, q_done)
            pe.wait_ge(w_ready, 1)
            pe.wait_ge(c_ready, 1)
            pe.wait_ge(k_ready, 1)
            project_rows(BK, cTh[:, 0], cTl[:, 0], WV, v_done)
            pe.wait_ge(maskb_ready, 1 + HC)
            pe.wait_ge(above_ready, 2)
            attend(0, 0, first=True)
            pe.wait_ge(w_ready, 2)
            attend(1, 1, second=True)
            attend(2, 0, third=True)
            with pe.Fori(1, (NB - 1) // 2) as i:
                b = i * 2 + 1
                attend(b, 1)
                attend(b + 1, 0)
            attend(NB - 1, 1, final=True)
            pe.wait_ge(pT_ready, NB * NC - 2)
            weigh_v(1, 1)
            pe.wait_ge(p_ready, NB * NC - 1)
            transpose_p(2)
            pe.wait_ge(on_ready, NB - 1)
            transpose_on()
            pe.wait_ge(pT_ready, NB * NC - 1)
            weigh_v(1, 2)
            pe.wait_ge(p_ready, NB * NC)
            transpose_p(3)
            pe.wait_ge(onTl_ready, NB - 1)
            pe.wait_ge(x1_ready, NB - 2)
            project_rows(BY, onTh, onTl, WO, y_done)
            pe.wait_ge(pT_ready, NB * NC)
            weigh_v(1, 3)
            pe.wait_ge(oT_ready, NB)
            transpose_o()
            pe.wait_ge(on_ready, NB)
            transpose_on()
            pe.wait_ge(onTl_ready, NB)
            pe.wait_ge(x1_ready, NB - 1)
            project_rows(BY, onTh, onTl, WO, y_done)

            BR, BL, BP = bank[0], bank[1], bank[2]
            BD = ((bank[3], bank[4]), (bank[5], bank[6]))

            def transpose_r(k4):
                for h in range(KH):
                    last = pe.transpose(BR[:, h * P:(h + 1) * P], xn[:, k4, h * P:(h + 1) * P], ident)
                last.then_inc(rT_done, 1)

            def logits():
                for h in range(KH):
                    last = pe.matmul(BL[:, 0:P], ctrl_sb[:, h, :], rT[:, h, :], start=(h == 0), stop=(h == KH - 1))
                last.then_inc(lg_done, 1)

            def route(b, k4, first=False, early=False, left=NB):
                k = k4 % 2
                pe.wait_ge(perm_ready, b + 1)
                if not first:
                    pe.wait_ge(pm_ready, b)
                pe.transpose(BP[:, 0:P], pc[:, k, :], ident).then_inc(pm_done, 1)
                if left > 1:
                    pe.wait_ge(rT_ready, b + 2)
                    pe.wait_ge(lt_ready, b + 1)
                    logits()
                if left > 2:
                    pe.wait_ge(rn_ready, b + 3)
                    transpose_r((k4 + 2) % 4)
                pe.wait_ge(pm_ready, b + 1)
                pe.wait_ge(rl_ready, b + 1)
                if not early:
                    pe.wait_ge(d_kept, b - 1)
                for h in range(KH):
                    for q, part in enumerate((rh, rl)):
                        last = pe.matmul(BD[k][h][:, :], part[:, k4, h * P:(h + 1) * P],
                                         permb[:, :, :].rearrange("p g s -> p (g s)"), start=(q == 0), stop=(q == 1))
                last.then_inc(d_done, 1)

            pe.wait_ge(small_loaded, 32)
            pe.wait_ge(rn_ready, 1)
            pe.wait_ge(x1_ready, NB)
            transpose_r(0)
            pe.wait_ge(rT_ready, 1)
            logits()
            pe.wait_ge(rn_ready, 2)
            transpose_r(1)
            for b in range(4):
                route(b, b, first=(b == 0), early=(b < 2))
            with pe.Fori(1, (NB - 4) // 4) as i:
                b = i * 4
                for k4 in range(4):
                    route(b + k4, k4)
            for k4 in range(4):
                route(NB - 4 + k4, k4, left=4 - k4)

            BH, BE = bank[0:2], bank[2:4]

            def expert_in(k4):
                k = k4 % 2
                for s in range(NS):
                    for h in range(KH):
                        last = pe.matmul(BH[k][s * F:(s + 1) * F, 0:GROUPS],
                                         wx[:, k4, h * P + s * F:h * P + (s + 1) * F], xe[:, k, h, s, :],
                                         start=(h == 0), stop=(h == KH - 1), tile_position=(0, s * F))
                last.then_inc(h_done, 1)

            def expert_out(k4):
                k = k4 % 2
                for h in range(KH):
                    last = pe.matmul(BE[k][:, h * E:(h + 1) * E], wx[:, k4, KH * P + h * P:KH * P + (h + 1) * P],
                                     hb[:, k].rearrange("p s g -> p (s g)"), start=True, stop=True)
                last.then_inc(e_done, 1)

            def expert(e, k4, loads, first=False, final=False):
                if not final:
                    pe.wait_ge(wx_loaded[(k4 + 1) % 4], loads)
                    pe.wait_ge(xe_ready, e + 2)
                    if not first:
                        pe.wait_ge(h_ready, e)
                    expert_in((k4 + 1) % 4)
                pe.wait_ge(h_ready, e + 1)
                if not isinstance(e, int) or e >= 2:
                    pe.wait_ge(e_kept, e - 1)
                expert_out(k4)

            pe.wait_ge(d_kept, NB)
            pe.wait_ge(wx_loaded[0], 16)
            pe.wait_ge(xe_ready, 1)
            expert_in(0)
            for e in range(4):
                expert(e, e, 16 if e < 3 else 32, first=(e == 0))
            with pe.Fori(1, (NE - 4) // 4) as i:
                e = i * 4
                for k4 in range(4):
                    expert(e + k4, k4, e * 4 + (16 if k4 < 3 else 32))
            for k4 in range(4):
                expert(NE - 4 + k4, k4, 16 * (NE // 4), final=(k4 == 3))

            BY2, BC = (bank[4:6], bank[6:8]), bank[0:2]

            def transpose_y(k):
                for g in range(NG):
                    for h in range(KH):
                        o = (g % 2) * E + h * P
                        last = pe.transpose(BY2[k][g // 2][:, o:o + P], yg[:, k, h, g, :], ident)
                last.then_inc(yT_done, 1)

            def combine(b, k, early=False, final=False):
                if not final:
                    pe.wait_ge(yg_ready, b + 2)
                    if not isinstance(b, int) or b >= 1:
                        pe.wait_ge(ys_ready, b)
                    transpose_y(1 - k)
                pe.wait_ge(ys_ready, b + 1)
                pe.wait_ge(pg_ready, b + 1)
                if not early:
                    pe.wait_ge(yo_ready, b - 1)
                for g in range(NG):
                    last = pe.matmul(BC[k][g * T:(g + 1) * T, 0:E], pg[:, k, g * T:(g + 1) * T],
                                     ys[:, k, g, :], start=True, stop=True, tile_position=(0, g * T))
                last.then_inc(c_done, 1)

            pe.wait_ge(e_kept, NE)
            pe.wait_ge(yg_ready, 1)
            transpose_y(0)
            combine(0, 0, early=True)
            combine(1, 1, early=True)
            with pe.Fori(1, (NB - 2) // 2) as i:
                b = i * 2
                for k in range(2):
                    combine(b + k, k)
            combine(NB - 2, 0)
            combine(NB - 1, 1, final=True)

        @block.scalar
        def _(act):
            for i in range(4):
                act.dma_start(w[:, i], wattn[:, i]).then_inc(w_loaded[i], 16)
            act.dma_start(cf[:, :], constf).then_inc(consts_loaded, 16)
            act.dma_start(gates_sb[:, :], gates).then_inc(gates_loaded, 16)
            act.dma_start(bo_sb[:, :], bo).then_inc(gates_loaded, 16)
            act.wait_ge(gates_loaded, 32)
            act.activation(tg[:, :], gates_sb[:, :], ACT.Tanh).then_inc(tanh_ready, 1)
            act.wait_ge(var_ready, 1)
            act.activation(sd[:, :], ve[:, :], ACT.Sqrt).then_inc(sd_ready, 1)

            def keep_x():
                act.activation(xT[:, :, :], BX[:, 0:E].rearrange("p (h t) -> p h t", h=KH), ACT.Copy)\
                    .then_inc(xT_ready, 1)

            def keep_q(k):
                for r in range(2):
                    last = act.activation(qz[64 * r:64 * r + 64, k, :, r, :],
                                          BQ[64 * r:64 * r + 64, 0:E].rearrange("p (h t) -> p h t", h=KH),
                                          ACT.Copy, scale=float(D) ** -0.5)
                last.then_inc(q_ready, 1)

            def keep_v(k):
                act.activation(va[:, k, :, 0:D], BK[:, 0:E].rearrange("p (h d) -> p h d", h=H), ACT.Copy)\
                    .then_inc(v_ready, 1)

            def keep_oT():
                act.activation(oT[:, :], BO[:, :], ACT.Copy).then_inc(oT_ready, 1)

            def keep_onT():
                act.activation(onTh[:, :, :], BQ[:, 0:E].rearrange("p (h t) -> p h t", h=KH), ACT.Copy)\
                    .then_inc(onTh_ready, 1)

            def context_high(k):
                act.activation(cTh[:, k], cT[:, k], ACT.Copy).then_inc(c_high, 1)

            def softmax(b, k, loads=None, first=False, second=False, final=False):
                for c in range(NC):
                    n = b * NC + c
                    act.wait_ge(max_ready, n + 1)
                    if not first or c >= 2:
                        act.wait_ge(pT_done, n - 1)
                    for j in range(HC):
                        last = act.activation(pr[:, c % 2, j, :], BS[c % 2][:, j * P:(j + 1) * P], ACT.Exp,
                                              bias=nmax[:, c * HC + j:c * HC + j + 1])
                    last.then_inc(p_ready, 1)
                    if c == 0 and not first and not second:
                        act.wait_ge(onT_done, b - 1)
                        keep_onT()
                    if c == 1 and not final:
                        act.wait_ge(xT_done, b + 2)
                        keep_x()
                    if c == 2:
                        if not first:
                            act.wait_ge(av_done, b * NC)
                            keep_oT()
                        if not final:
                            act.wait_ge(q_done, b + 2)
                            keep_q(1 - k)
                    if c == 3:
                        if not final:
                            act.wait_ge(v_done, b + 2)
                            keep_v(1 - k)
                        if loads is not None:
                            act.wait_ge(ctx_loaded[k], loads)
                            context_high(k)

            for k in range(2):
                act.wait_ge(ctx_loaded[k], 16)
                context_high(k)
            act.wait_ge(xT_done, 1)
            keep_x()
            act.wait_ge(q_done, 1)
            act.wait_ge(zeroed, 2)
            keep_q(0)
            act.wait_ge(v_done, 1)
            keep_v(0)
            softmax(0, 0, 32, first=True)
            softmax(1, 1, 32, second=True)
            softmax(2, 0, 48)
            with act.Fori(1, NB // 2 - 2) as i:
                b = i * 2 + 1
                for k in range(2):
                    softmax(b + k, 1 - k, i * 16 + (32 + 16 * k))
            softmax(NB - 3, 1, 16 * (NB // 2))
            softmax(NB - 2, 0)
            softmax(NB - 1, 1, final=True)
            act.wait_ge(onT_done, NB - 1)
            keep_onT()
            act.wait_ge(av_done, NB * NC)
            keep_oT()
            act.wait_ge(onT_done, NB)
            keep_onT()
            act.wait_ge(var_ready, 2)
            act.activation(sd[:, :], ve[:, :], ACT.Sqrt).then_inc(sd_ready, 1)

            def keep_r():
                act.activation(rT[:, :, :], bank[0][:, 0:E].rearrange("p (h t) -> p h t", h=KH), ACT.Copy)\
                    .then_inc(rT_ready, 1)

            def keep_d(b, k):
                act.wait_ge(d_done, b + 1)
                for h in range(KH):
                    last = act.activation(routed[:, h, bass.ds(b * NG, NG), :],
                                          bank[3 + 2 * k + h][:, :].rearrange("p (g s) -> p g s", g=NG), ACT.Copy)
                last.then_inc(d_kept, 1)

            def rows_high(b, k4):
                act.wait_ge(rn_ready, b + 1)
                act.activation(rh[:, k4], xn[:, k4], ACT.Copy).then_inc(rh_ready, 1)

            def route(b, k4, left=NB):
                if left > 2:
                    rows_high(b + 2, (k4 + 2) % 4)
                    act.wait_ge(rT_done, b + 3)
                    keep_r()
                keep_d(b, k4 % 2)

            for b in range(2):
                rows_high(b, b)
                act.wait_ge(rT_done, b + 1)
                keep_r()
            with act.Fori(0, NB // 4 - 1) as i:
                b = i * 4
                for k4 in range(4):
                    route(b + k4, k4)
            for k4 in range(4):
                route(NB - 4 + k4, k4, left=4 - k4)

            with act.Fori(0, NE // 2) as i:
                e = i * 2
                for k in range(2):
                    act.wait_ge(e_done, e + (k + 1))
                    act.activation(routed[:, :, :, bass.ds((e + k) * NS, NS)],
                                   bank[2 + k][:, :].rearrange("p (h s g) -> p h g s", h=KH, s=NS), ACT.Copy)\
                        .then_inc(e_kept, 1)

            with act.Fori(0, NB // 2) as i:
                b = i * 2
                for k in range(2):
                    act.wait_ge(yT_done, b + (k + 1))
                    for q in range(2):
                        last = act.activation(ys[:, k, 2 * q:2 * q + 2, :],
                                              bank[4 + 2 * k + q][:, :].rearrange("p (g e) -> p g e", g=2), ACT.Copy)
                    last.then_inc(ys_ready, 1)

        @block.vector
        def _(dve):
            def rstd(step):
                n = 5 * step
                dve.wait_ge(sd_ready, step + 1)
                dve.reciprocal(rs[:, :], sd[:, :]).then_inc(rs_step, 1)
                dve.wait_ge(rs_step, n + 1)
                dve.tensor_tensor(nt[:, :], ve[:, :], rs[:, :], ALU.mult).then_inc(rs_step, 1)
                dve.wait_ge(rs_step, n + 2)
                dve.tensor_tensor(nt[:, :], nt[:, :], rs[:, :], ALU.mult).then_inc(rs_step, 1)
                dve.wait_ge(rs_step, n + 3)
                dve.tensor_scalar(nt[:, :], nt[:, :], -0.5, 1.5, ALU.mult, ALU.add).then_inc(rs_step, 1)
                dve.wait_ge(rs_step, n + 4)
                dve.tensor_tensor(rs[:, :], rs[:, :], nt[:, :], ALU.mult).then_inc(rs_step, 1)
                dve.wait_ge(rs_step, n + 5)

            def moments(step):
                n = 4 * step
                mean, half = mv[:, :, 0], mv[:, :, 1]
                dve.tensor_tensor(mean, stats[:, :, 1], stats[:, :, 4], ALU.add).then_inc(mom_step, 1)
                dve.tensor_tensor(half, stats[:, :, 1], stats[:, :, 4], ALU.subtract).then_inc(mom_step, 1)
                dve.tensor_tensor(ve[:, :], stats[:, :, 2], stats[:, :, 5], ALU.add).then_inc(mom_step, 1)
                dve.wait_ge(mom_step, n + 3)
                dve.tensor_scalar(mean, mean, 0.5, None, ALU.mult)
                dve.tensor_tensor(half, half, half, ALU.mult)
                dve.tensor_scalar(ve[:, :], ve[:, :], 1.0 / E, EPS, ALU.mult, ALU.add).then_inc(mom_step, 1)
                dve.wait_ge(mom_step, n + 4)
                dve.scalar_tensor_tensor(ve[:, :], half, 0.25, ve[:, :], ALU.mult, ALU.add).then_inc(var_ready, 1)

            for c in range(2):
                dve.memset(BS[c][:, :], NEG).then_inc(above_ready, 1)
            for i in range(NB // XC):
                dve.wait_ge(x_loaded[i], 16)
                for b in range(i * XC, (i + 1) * XC):
                    last = dve.bn_stats(stats[:, b, :], xs[:, b, :])
            last.then_inc(stats_ready, 1)
            dve.wait_ge(stats_ready, 1)
            moments(0)
            dve.wait_ge(gates_loaded, 32)
            dve.wait_ge(tanh_ready, 1)
            dve.tensor_scalar(bo_sb[:, :], bo_sb[:, :], tg[:, 0:1], None, ALU.mult).then_inc(bo_ready, 1)
            rstd(0)
            def split_weight(m):
                dve.wait_ge(w_loaded[2 + m], 16)
                dve.tensor_copy(wh[:, m], w[:, 2 + m]).then_inc(w_high, 1)
                dve.wait_ge(w_high, m + 1)
                dve.tensor_tensor(wl[:, m], w[:, 2 + m], wh[:, m].bitcast(F32), ALU.subtract).then_inc(w_ready, 1)

            def normalize(b, k, ready):
                dve.tensor_scalar(xn[:, k, :], xs[:, b, :], mv[:, b, 0:1], rs[:, bass.ds(b, 1)],
                                  ALU.subtract, ALU.mult).then_inc(ready, 1)

            def keep_k(k, h):
                return dve.tensor_tensor(kd[:, k, h], BK[:, None, h * P:(h + 1) * P].to_broadcast([P, HC, P]),
                                         headmask[:, :, None].to_broadcast([P, HC, P]), ALU.mult)

            def normalize_o(count):
                o = BX[:, :].rearrange("p (h r) -> p h r", h=H)
                dve.reciprocal(rsum[:, :], o[:, :, D]).then_inc(rsum_ready, 1)
                dve.wait_ge(rsum_ready, count)
                dve.tensor_tensor(on[:, :].rearrange("p (h d) -> p h d", h=H), o[:, :, 0:D],
                                  rsum[:, :, None].to_broadcast([P, H, D]), ALU.mult).then_inc(on_ready, 1)

            def low_part(low, high, bank_, ready):
                dve.tensor_tensor(low[:, :, :], bank_[:, 0:E].rearrange("p (h t) -> p h t", h=KH),
                                  high[:, :, :].bitcast(F32), ALU.subtract).then_inc(ready, 1)

            def residual(b):
                dve.scalar_tensor_tensor(xs[:, b, :], BY[:, 0:E], tg[:, 0:1], xs[:, b, :], ALU.mult, ALU.add)\
                    .then_inc(x1_ready, 1)

            def keep_pT(c):
                dve.tensor_copy(pT[:, c % 2, :], BT[:, :]).then_inc(pT_ready, 1)

            def attend(b, k, first=False, second=False, last_but_one=False, final=False):
                late = not first and not second
                for c in range(NC):
                    n = b * NC + c
                    if c == 0 and late:
                        dve.wait_ge(o_done, b - 1)
                        normalize_o(b - 1)
                    dve.wait_ge(s_done, n + 1)
                    dve.tensor_reduce(nmax[:, c * HC:(c + 1) * HC], BS[c % 2][:, :].rearrange("p (j t) -> p j t", j=HC),
                                      AX_X, ALU.max, negate=True).then_inc(max_ready, 1)
                    if c == 1 and late:
                        dve.wait_ge(onTh_ready, b - 1)
                        low_part(onTl, onTh, BQ, onTl_ready)
                    if not first or c >= 2:
                        dve.wait_ge(pT_done, n - 1)
                        keep_pT(c)
                    if c == 0 and not final:
                        dve.wait_ge(k_done, b + 2)
                        keep_k(1 - k, 0)
                    if c == 1 and not final:
                        keep_k(1 - k, 1).then_inc(k_ready, 1)
                    if c == 2 and late:
                        dve.wait_ge(y_done, b - 1)
                        dve.wait_ge(xb_ready, b - 1)
                        residual(b - 2)
                        dve.wait_ge(x1_ready, b - 1)
                        dve.bn_stats(stats[:, b - 2, :], xs[:, b - 2, :])
                    if c == 3 and not final and not last_but_one:
                        dve.wait_ge(xT_done, b + 2)
                        normalize(b + 2, 0, xn_ready)

            normalize(0, 0, xn_ready)
            dve.wait_ge(consts_loaded, 16)
            dve.wait_ge(k_done, 1)
            keep_k(0, 0)
            keep_k(0, 1).then_inc(k_ready, 1)
            split_weight(0)
            dve.wait_ge(xT_done, 1)
            normalize(1, 0, xn_ready)
            split_weight(1)
            attend(0, 0, first=True)
            attend(1, 1, second=True)
            with dve.Fori(1, (NB - 2) // 2) as i:
                b = i * 2
                for k in range(2):
                    attend(b + k, k)
            attend(NB - 2, 0, last_but_one=True)
            attend(NB - 1, 1, final=True)
            dve.wait_ge(o_done, NB - 1)
            normalize_o(NB - 1)
            dve.wait_ge(pT_done, NB * NC - 1)
            keep_pT(2)
            dve.wait_ge(onTh_ready, NB - 1)
            low_part(onTl, onTh, BQ, onTl_ready)
            dve.wait_ge(pT_done, NB * NC)
            keep_pT(3)
            for b in (NB - 2, NB - 1):
                if b == NB - 1:
                    dve.wait_ge(o_done, NB)
                    normalize_o(NB)
                    dve.wait_ge(onTh_ready, NB)
                    low_part(onTl, onTh, BQ, onTl_ready)
                dve.wait_ge(y_done, b + 1)
                dve.wait_ge(xb_ready, b + 1)
                residual(b)
                dve.wait_ge(x1_ready, b + 1)
                last = dve.bn_stats(stats[:, b, :], xs[:, b, :])
            last.then_inc(stats_ready, 1)
            dve.wait_ge(stats_ready, 2)
            moments(1)
            rstd(1)

            def choose(b, k, early):
                dve.wait_ge(lg_done, b + 1)
                dve.tensor_tensor(lt[:, :], bank[1][:, 0:P], tie, ALU.add).then_inc(lt_ready, 1)
                dve.wait_ge(lt_ready, b + 1)
                lg = lt[:, :].rearrange("p (g t) -> p g t", g=NG)
                dve.tensor_reduce(gmax[:, :], lg, AX_X, ALU.max).then_inc(gmax_ready, 1)
                dve.wait_ge(gmax_ready, b + 1)
                if not early:
                    dve.wait_ge(permT_kept, b - 1)
                dve.tensor_tensor(pc[:, k, :].rearrange("p (g t) -> p g t", g=NG), lg,
                                  gmax[:, :, None].to_broadcast([P, NG, T]), ALU.is_equal).then_inc(perm_ready, 1)

            def spread(b):
                dve.wait_ge(pm_done, b + 1)
                dve.tensor_tensor(permb[:, :, :], bank[2][:, None, 0:P].to_broadcast([P, NG, P]),
                                  groupmask[:, :, None].to_broadcast([P, NG, P]), ALU.mult).then_inc(pm_ready, 1)

            def route(b, k4, left=NB):
                spread(b)
                if left > 1:
                    choose(b + 1, (k4 + 1) % 2, isinstance(b, int) and b == 0)
                if left > 3:
                    normalize(b + 3, (k4 + 3) % 4, rn_ready)

            for b in range(3):
                normalize(b, b, rn_ready)
            choose(0, 0, True)
            for b in range(4):
                route(b, b)
            with dve.Fori(1, (NB - 4) // 4) as i:
                b = i * 4
                for k4 in range(4):
                    route(b + k4, k4)
            for k4 in range(4):
                route(NB - 4 + k4, k4, left=4 - k4)

            def stage(e, k):
                dve.tensor_copy(xe[:, k].rearrange("p h s g -> p h g s"),
                                routed[:, :, :, bass.ds(e * NS, NS)]).then_inc(xe_ready, 1)

            def hidden(e, k):
                for s in range(NS):
                    r = slice(s * F, (s + 1) * F)
                    last = dve.tensor_scalar(hb[r, k, s, :], bank[k][r, 0:GROUPS], ebias_sb[r, bass.ds(e, 1)], 0.0,
                                             ALU.add, ALU.max)
                last.then_inc(h_ready, 1)

            dve.wait_ge(d_kept, NB)
            stage(0, 0)
            stage(1, 1)
            dve.wait_ge(zeroed, 3)
            for e in range(2):
                dve.wait_ge(h_done, e + 1)
                hidden(e, e)
                stage(e + 2, e)
            with dve.Fori(1, (NE - 2) // 2) as i:
                e = i * 2
                for k in range(2):
                    dve.wait_ge(h_done, e + (k + 1))
                    dve.wait_ge(e_done, e + (k - 1))
                    hidden(e + k, k)
                    stage(e + (k + 2), k)
            for k in range(2):
                dve.wait_ge(h_done, NE - 1 + k)
                dve.wait_ge(e_done, NE - 3 + k)
                hidden(NE - 2 + k, k)

            def stage_y(b, k):
                dve.tensor_copy(yg[:, k], routed[:, :, bass.ds(b * NG, NG), :]).then_inc(yg_ready, 1)

            def finish(b, k):
                dve.wait_ge(c_done, b + 1)
                dve.scalar_tensor_tensor(yo[:, k, :], bank[k][:, 0:E], tg[:, 1:2], xs[:, b, :], ALU.mult, ALU.add)\
                    .then_inc(yo_ready, 1)

            dve.wait_ge(e_kept, NE)
            stage_y(0, 0)
            stage_y(1, 1)
            for k in range(2):
                dve.wait_ge(yT_done, k + 1)
                stage_y(k + 2, k)
                finish(k, k)
            with dve.Fori(1, (NB - 2) // 2) as i:
                b = i * 2
                for k in range(2):
                    dve.wait_ge(yT_done, b + (k + 1))
                    stage_y(b + (k + 2), k)
                    dve.wait_ge(stored[k], b * 8)
                    finish(b + k, k)
            for k in range(2):
                dve.wait_ge(stored[k], 8 * (NB - 2))
                finish(NB - 2 + k, k)


def constants():
    import numpy as np

    rows = np.arange(P)
    ident = np.eye(P, dtype=np.float32)
    heads = ((rows[:, None] // D) % HC == np.arange(HC)[None, :]).astype(np.float32)
    step = np.arange(T, dtype=np.float32) * (np.float32(1e-6) / np.float32(T - 1))
    ramp = np.broadcast_to(np.tile(step, NG)[None, :], (P, P))
    groups = (rows[:, None] // T == np.arange(NG)[None, :]).astype(np.float32)
    mask = np.where(np.arange(DP)[None, :] <= rows[:, None] % DP, 0.0, NEG).astype(np.float32)
    return np.concatenate([ident, heads, ramp, groups, mask], axis=1)


def kernel(**inputs):
    import numpy as _np
    import concourse.bacc as _bacc
    from concourse import mybir as _mybir
    from concourse.bass_utils import run_bass_kernel_spmd as _run

    a = {name: _np.asarray(v) for name, v in inputs.items()}

    def halves(m):
        return m.reshape(KH, P, -1).transpose(1, 0, 2)

    f1 = a["L0_ffn_f1"].reshape(KH, P, NE, NS * F).transpose(2, 1, 0, 3).reshape(NE, P, KH * NS * F)
    f2 = a["L0_ffn_f2"].reshape(NE, NS * F, E)
    laid = {
        "x": a["x"],
        "ctxT": a["ctx_1024"].reshape(NB, P, KH, P).transpose(0, 3, 2, 1),
        "wattn": _np.stack([halves(a["L0_xattn_" + n].T) for n in ("Wk", "Wq", "Wv", "Wo")], axis=1),
        "bo": _np.broadcast_to(a["L0_xattn_bo"], (P, E)),
        "gates": _np.broadcast_to(_np.concatenate([a["g_xattn"], a["g_ffn"]]), (P, 2)),
        "ctrl": halves(a["L0_ffn_controller"].reshape(E, SLOTS)),
        "wexp": _np.concatenate([f1, f2], axis=2),
        "ebias": a["L0_ffn_bias"].reshape(NE, NS * F).T,
        "constf": constants(),
    }
    nc = _bacc.Bacc("TRN2", target_bir_lowering=False, num_devices=1)
    arrays, args = {}, []
    for name, v in laid.items():
        v = _np.ascontiguousarray(v)
        arrays[f"in_{name}_dram"] = v
        args.append(nc.dram_tensor(f"in_{name}_dram", v.shape, _mybir.dt.from_np(v.dtype), kind="ExternalInput").ap())
    args.append(nc.dram_tensor("out_0_dram", (NB, P, E), F32, kind="ExternalOutput").ap())
    build(nc, *args)
    r = _run(nc, [arrays], core_ids=[0])
    return r.results[0]["out_0_dram"]
```

```python
from contextlib import ExitStack

import concourse.bass as bass
from concourse import mybir

F32 = mybir.dt.float32
F32R = mybir.dt.float32r
I32 = mybir.dt.int32
BF16 = mybir.dt.bfloat16
ALU = mybir.AluOpType
ACT = mybir.ActivationFunctionType
AX_X = mybir.AxisListType.X

P = 128
NB = 16
E = 256
KH = E // P
H = 16
D = E // H
HC = 4
NC = H // HC
DP = 32
VP = 3 * D
NE, NS, F = 32, 4, 32
SLOTS = NE * NS
T = 32
NG = P // T
GROUPS = NB * NG
RING = 8
XR = 4
XC = 4
RSTD_STAGES = 13
EPS = 1e-5
RSQRT_SEED = float(0x5F3759DF)
NEG = -(2.0 ** 100)


def build(nc, x, ctxT, wattn, gbo, ctrl, wexp, constf, out):
    with ExitStack() as ctx:
        def sb(name, shape, dt=F32):
            return ctx.enter_context(nc.sbuf_tensor(name, shape, dt))

        def sem(name):
            return ctx.enter_context(nc.semaphore(name))

        bank = [ctx.enter_context(nc.psum_tensor(f"bank{i}", [P, 512], F32)) for i in range(8)]

        cf = sb("cf", [P, P + HC + P + NG + DP])
        ident = cf[:, 0:P]
        headmask = cf[:, P:P + HC]
        tie = cf[:, P + HC:P + HC + P]
        groupmask = cf[:, P + HC + P:P + HC + P + NG]
        mask = cf[:, P + HC + P + NG:P + HC + P + NG + DP]
        cb = sb("cb", [P, P + HC * DP], BF16)
        identb = cb[:, 0:P]
        causal = cb[:, P:P + HC * DP]
        w = sb("w", [P, 4, KH, E])
        wh = sb("wh", [P, 2, KH, E], F32R)
        wl = sb("wl", [P, 2, KH, E], F32R)
        wk, wq, WV, WO = w[:, 0], w[:, 1], 0, 1
        gb = sb("gb", [P, 2 + E])
        gates_sb, bo_sb = gb[:, 0:2], gb[:, 2:]
        tg = sb("tg", [P, 2])
        ctrl_sb = sb("ctrl_sb", [P, KH, SLOTS])

        xs = sb("xs", [P, NB, E])
        stats = sb("stats", [P, NB, 6])
        mv = sb("mv", [P, NB, 2])
        ve = sb("ve", [P, NB])
        rs = sb("rs", [P, NB])
        nt = sb("nt", [P, NB])
        warm = sb("warm", [P, 1])
        xn = sb("xn", [P, 4, E])
        xT = sb("xT", [P, KH, P])
        cTh = sb("cTh", [P, 2, KH, P], F32R)
        cTl = sb("cTl", [P, 2, KH, P], F32R)
        cT = sb("cT", [P, 2, KH, P])
        kd = sb("kd", [P, 2, KH, HC, P])
        qz = sb("qz", [P, 2, KH, 2, P])
        va = sb("va", [P, 2, H, VP])
        nmax = sb("nmax", [P, H])
        pr = sb("pr", [P, 2, HC, P])
        pT = sb("pT", [P, 2, HC * P])
        psum = sb("psum", [P, H])
        rsum = sb("rsum", [P, H])
        onTh = sb("onTh", [P, KH, P], F32R)
        onTl = sb("onTl", [P, KH, P], F32R)

        rT = sb("rT", [P, KH, P])
        rh = sb("rh", [P, 4, E], F32R)
        rl = sb("rl", [P, 4, E], F32R)
        lt = sb("lt", [P, P])
        gmax = sb("gmax", [P, NG])
        pc = sb("pc", [P, 2, P])
        permT = sb("permT", [P, NB, P])
        permb = sb("permb", [P, 2, NG, P], F32R)
        routed = sb("routed", [P, KH, GROUPS, SLOTS])
        wx = sb("wx", [P, RING, KH * P + E + 1])
        xe = sb("xe", [P, XR, KH, NS, GROUPS])
        hb = sb("hb", [P, 2, NS, GROUPS])
        yg = sb("yg", [P, 2, KH, NG, SLOTS])
        pg = sb("pg", [P, 2, P])
        ys = sb("ys", [P, 2, NG, E])

        x_loaded = [sem(f"x_loaded{i}") for i in range(NB // XC)]
        consts_loaded = sem("consts_loaded")
        maskb_ready = sem("maskb_ready")
        small_loaded = sem("small_loaded")
        gates_loaded = sem("gates_loaded")
        w_loaded = [sem(f"w_loaded{i}") for i in range(4)]
        ctx_loaded = [sem(f"ctx_loaded{i}") for i in range(2)]
        wx_loaded = [sem(f"wx_loaded{i}") for i in range(RING)]
        stored = sem("stored")
        zeroed = sem("zeroed")
        above_ready = sem("above_ready")
        w_high = sem("w_high")
        w_ready = sem("w_ready")
        dve_step = sem("dve_step")
        act_warm = sem("act_warm")
        stats_ready = sem("stats_ready")
        tanh_ready = sem("tanh_ready")
        bo_ready = sem("bo_ready")
        xn_ready = sem("xn_ready")
        xT_done = sem("xT_done")
        xT_ready = sem("xT_ready")
        c_high = sem("c_high")
        c_ready = sem("c_ready")
        k_done = sem("k_done")
        k_ready = sem("k_ready")
        q_done = sem("q_done")
        q_ready = sem("q_ready")
        v_done = sem("v_done")
        v_ready = sem("v_ready")
        onTh_ready = sem("onTh_ready")
        onTl_ready = sem("onTl_ready")
        y_done = sem("y_done")
        xb_ready = sem("xb_ready")
        x1_ready = sem("x1_ready")
        s_done = sem("s_done")
        max_ready = sem("max_ready")
        p_ready = sem("p_ready")
        rsum_ready = sem("rsum_ready")
        pn_ready = sem("pn_ready")
        pT_done = sem("pT_done")
        pT_ready_act = sem("pT_ready_act")
        pT_ready_dve = sem("pT_ready_dve")
        av_done = sem("av_done")
        rn_ready = sem("rn_ready")
        rh_ready = sem("rh_ready")
        rl_ready = sem("rl_ready")
        rT_done = sem("rT_done")
        rT_ready = sem("rT_ready")
        lg_done = sem("lg_done")
        lt_ready = sem("lt_ready")
        gmax_ready = sem("gmax_ready")
        perm_ready = sem("perm_ready")
        pm_done = sem("pm_done")
        pm_ready = sem("pm_ready")
        d_done = sem("d_done")
        d_kept = sem("d_kept")
        d_kept_dve = sem("d_kept_dve")
        xe_ready = sem("xe_ready")
        h_done = sem("h_done")
        h_ready = sem("h_ready")
        e_done = sem("e_done")
        e_kept = sem("e_kept")
        permT_kept = sem("permT_kept")
        yg_ready = sem("yg_ready")
        pg_ready = sem("pg_ready")
        yT_done = sem("yT_done")
        ys_ready = sem("ys_ready")
        c_done = sem("c_done")
        yo_ready = sem("yo_ready")

        BS, BT, BO, BK, BQ, BY = bank[0:2], bank[2], bank[3:5], bank[5], bank[6], bank[7]
        XQ = BQ[:, E:2 * E]

        block = ctx.enter_context(nc.Block())

        @block.sync
        def _(sp):
            sp.dma_start(cT[:, 0], ctxT[0]).then_inc(ctx_loaded[0], 16)
            for i in range(NB // XC):
                lo, hi = i * XC, (i + 1) * XC
                sp.dma_start(xs[:, lo:hi, :], x[lo:hi].rearrange("b s e -> s b e")).then_inc(x_loaded[i], 16)
                if i == 0:
                    sp.dma_start(cT[:, 1], ctxT[1]).then_inc(ctx_loaded[1], 16)
            sp.dma_start(ctrl_sb[:, :, :], ctrl).then_inc(small_loaded, 16)
            for r in range(RING):
                sp.dma_start(wx[:, r], wexp[r]).then_inc(wx_loaded[r], 16)
            with sp.Fori(1, NB // 2) as i:
                b = i * 2
                for k in range(2):
                    sp.wait_ge(c_ready, b + (k - 1))
                    sp.wait_ge(k_done, b + (k - 1))
                    sp.dma_start(cT[:, k], ctxT[b + k]).then_inc(ctx_loaded[k], 16)
            with sp.Fori(1, NE // RING) as i:
                e = i * RING
                for r in range(RING):
                    sp.wait_ge(e_done, e + (r - RING + 1))
                    sp.dma_start(wx[:, r], wexp[e + r]).then_inc(wx_loaded[r], 16)
            with sp.Fori(0, NB // 2) as i:
                b = i * 2
                for k in range(2):
                    sp.wait_ge(yo_ready, b + (k + 1))
                    sp.dma_start(out[b + k], xs[:, b + k, :]).then_inc(stored, 16)
            sp.wait_ge(stored, 16 * NB)


        @block.gpsimd
        def _(pool):
            pool.memset(qz[:, :, :, :, :], 0.0).then_inc(zeroed, 1)
            pool.memset(va[:, :, :, :], 0.0).then_inc(zeroed, 1)
            pool.memset(hb[:, :, :, :], 0.0).then_inc(zeroed, 1)
            pool.wait_ge(consts_loaded, 16)
            pool.tensor_copy(identb, ident).then_inc(maskb_ready, 1)
            for j in range(HC):
                pool.tensor_copy(causal[:, j * DP:(j + 1) * DP], mask).then_inc(maskb_ready, 1)

            def split_context(k, n):
                pool.wait_ge(c_high, n)
                pool.tensor_tensor(cTl[:, k], cT[:, k], cTh[:, k].bitcast(F32), ALU.subtract).then_inc(c_ready, 1)

            def bias_x(b):
                pool.wait_ge(xn_ready, b + 1)
                pool.tensor_tensor(xs[:, b, :], xs[:, b, :], bo_sb[:, :], ALU.add).then_inc(xb_ready, 1)

            def attend(b, k, first=False, final=False):
                for c in range(NC):
                    pool.wait_ge(p_ready, b * NC + (c + 1))
                    pool.wait_ge(rsum_ready, b * NC + (c + 1))
                    pool.tensor_tensor(pr[:, c % 2], pr[:, c % 2],
                                       rsum[:, c * HC:(c + 1) * HC, None].to_broadcast([P, HC, P]), ALU.mult)\
                        .then_inc(pn_ready, 1)
                    if c == 0 and not first and not final:
                        split_context(1 - k, b + 2)
                    if c == 1 and not final:
                        bias_x(b + 1)

            for k in range(2):
                split_context(k, k + 1)
            pool.wait_ge(bo_ready, 1)
            bias_x(0)
            attend(0, 0, first=True)
            with pool.Fori(0, NB // 2 - 1) as i:
                b = i * 2 + 1
                attend(b, 1)
                attend(b + 1, 0)
            attend(NB - 1, 1, final=True)

            def split_rows(b, k4):
                pool.wait_ge(rh_ready, b + 1)
                pool.tensor_tensor(rl[:, k4], xn[:, k4], rh[:, k4].bitcast(F32), ALU.subtract).then_inc(rl_ready, 1)

            def keep_perm(b, k):
                pool.wait_ge(perm_ready, b + 1)
                pool.tensor_copy(permT[:, b, :], pc[:, k, :]).then_inc(permT_kept, 1)

            for b in range(3):
                split_rows(b, b)
            with pool.Fori(0, NB // 4 - 1) as i:
                b = i * 4
                for k4 in range(4):
                    keep_perm(b + k4, k4 % 2)
                    split_rows(b + (k4 + 3), (k4 + 3) % 4)
            for k4 in range(4):
                keep_perm(NB - 4 + k4, k4 % 2)
                if k4 < 1:
                    split_rows(NB - 1, 3)
            pool.wait_ge(permT_kept, NB)
            for k in range(2):
                pool.tensor_copy(pg[:, k, :], permT[:, k, :]).then_inc(pg_ready, 1)
            with pool.Fori(1, NB // 2) as i:
                b = i * 2
                for k in range(2):
                    pool.wait_ge(c_done, b + (k - 1))
                    pool.tensor_copy(pg[:, k, :], permT[:, b + k, :]).then_inc(pg_ready, 1)

        @block.tensor
        def _(pe):
            def transpose_x(b, k):
                for h in range(KH):
                    last = pe.transpose(XQ[:, h * P:(h + 1) * P], xn[:, k, h * P:(h + 1) * P], ident)
                last.then_inc(xT_done, 1)

            def project(dst, weight, src, done):
                for o in range(KH):
                    for i in range(KH):
                        last = pe.matmul(dst[:, o * P:(o + 1) * P], weight[:, i, o * P:(o + 1) * P],
                                         src[:, i, :], start=(i == 0), stop=(i == KH - 1))
                last.then_inc(done, 1)

            def project_rows(dst, high, low, m, done):
                parts = [(src[:, i, :], wt[:, m, i, :])
                         for i in range(KH) for src, wt in ((high, wh), (low, wh), (high, wl))]
                for q, (stationary, moving) in enumerate(parts):
                    last = pe.matmul(dst[:, 0:E], stationary, moving, start=(q == 0), stop=(q == len(parts) - 1))
                last.then_inc(done, 1)

            def scores(k, c):
                bs = BS[c % 2][:, :].rearrange("p (h t) -> p h t", h=HC)
                for j in range(P // DP):
                    r = slice(j * DP, (j + 1) * DP)
                    pe.matmul(bs[r, :, r], identb[:, r], causal, start=True, stop=False,
                              tile_position=(0, j * DP), skip_group_check=True)
                for j in range(P // DP):
                    r = slice(j * DP, (j + 1) * DP)
                    last = pe.matmul(bs[r, :, 0:(j + 1) * DP], qz[:, k, c // 2, c % 2, r],
                                     kd[:, k, c // 2, :, 0:(j + 1) * DP], start=False, stop=True,
                                     tile_position=(0, j * DP), skip_group_check=True)
                last.then_inc(s_done, 1)

            def transpose_p(c):
                for j in range(HC):
                    last = pe.transpose(BT[:, j * P:(j + 1) * P], pr[:, c % 2, j, :], ident)
                last.then_inc(pT_done, 1)

            def weigh_v(k, c):
                odd = c % 2
                o = (c // 2) * P
                for j in range(HC):
                    last = pe.matmul(BO[k][j * DP:(j + 1) * DP, o:o + P], va[:, k, c * HC + j, D * (1 - odd):][:, 0:DP],
                                     pT[:, c % 2, j * P:(j + 1) * P], start=(odd == 0), stop=(odd == 1),
                                     tile_position=(0, j * DP), skip_group_check=True)
                last.then_inc(av_done, 1)

            BR, BL, BP = bank[0], bank[1], (bank[2], bank[7])
            BD = ((bank[5], bank[6]), (bank[3], bank[4]))

            def transpose_r(k4, to=BR):
                for h in range(KH):
                    last = pe.transpose(to[:, h * P:(h + 1) * P], xn[:, k4, h * P:(h + 1) * P], ident)
                last.then_inc(rT_done, 1)

            def logits(to=BL):
                for h in range(KH):
                    last = pe.matmul(to[:, 0:P], ctrl_sb[:, h, :], rT[:, h, :], start=(h == 0), stop=(h == KH - 1))
                last.then_inc(lg_done, 1)

            def spread(b, k, first=False):
                pe.wait_ge(perm_ready, b + 1)
                if not first:
                    pe.wait_ge(pm_ready, b - 1)
                pe.transpose(BP[k][:, 0:P], pc[:, k, :], ident).then_inc(pm_done, 1)

            def attend(b, k, first=False, second=False, third=False, final=False):
                for c in range(NC):
                    n = b * NC + c
                    if c == 0:
                        pe.wait_ge(q_ready, b + 1)
                        pe.wait_ge(k_ready, b + 1)
                    if not first or c >= 2:
                        pe.wait_ge(p_ready, n - 1)
                    scores(k, c)
                    if not first or c == 3:
                        if c == 0 or c == 3:
                            pe.wait_ge(pT_ready_dve, 2 * b + (0 if c == 0 else 1))
                        else:
                            pe.wait_ge(pT_ready_act, 2 * b + (c - 2))
                        if c == 3:
                            pe.wait_ge(v_ready, b + 1)
                            if not first and not second:
                                pe.wait_ge(onTl_ready, b - 1)
                        weigh_v(k if c == 3 else 1 - k, (c - 3) % NC)
                    if not first or c >= 2:
                        pe.wait_ge(pn_ready, n - 1)
                        transpose_p((c - 2) % NC)
                    if c == 0 and not final:
                        pe.wait_ge(c_high, b + 2)
                        pe.wait_ge(v_ready, b + 1)
                        project(BK, wk, cT[:, 1 - k], k_done)
                    if c == 1 and not first and not second:
                        pe.wait_ge(onTl_ready, b - 1)
                        if not third:
                            pe.wait_ge(x1_ready, b - 2)
                        project_rows(BY, onTh, onTl, WO, y_done)
                    if c == 1 and not final:
                        pe.wait_ge(xn_ready, b + 2)
                        transpose_x(b, 0)
                    if c == 2 and not final:
                        pe.wait_ge(xT_ready, b + 2)
                        project(BQ, wq, xT, q_done)
                    if final and c == 2:
                        pe.wait_ge(rn_ready, 1)
                        transpose_r(0, BQ)
                    if final and c == 3:
                        pe.wait_ge(small_loaded, 16)
                        pe.wait_ge(rT_ready, 1)
                        logits(BK)
                        pe.wait_ge(rn_ready, 2)
                        transpose_r(1, BQ)
                    if c == 3:
                        if not final:
                            pe.wait_ge(k_ready, b + 2)
                            pe.wait_ge(c_ready, b + 2)
                            project_rows(BK, cTh[:, 1 - k], cTl[:, 1 - k], WV, v_done)

            pe.wait_ge(w_loaded[0], 16)
            pe.wait_ge(c_high, 1)
            project(BK, wk, cT[:, 0], k_done)
            pe.wait_ge(consts_loaded, 16)
            pe.wait_ge(xn_ready, 1)
            transpose_x(0, 0)
            pe.wait_ge(w_loaded[1], 16)
            pe.wait_ge(xT_ready, 1)
            project(BQ, wq, xT, q_done)
            pe.wait_ge(w_ready, 1)
            pe.wait_ge(c_ready, 1)
            pe.wait_ge(k_ready, 1)
            project_rows(BK, cTh[:, 0], cTl[:, 0], WV, v_done)
            pe.wait_ge(maskb_ready, 1 + HC)
            pe.wait_ge(above_ready, 2)
            attend(0, 0, first=True)
            pe.wait_ge(w_ready, 2)
            attend(1, 1, second=True)
            attend(2, 0, third=True)
            with pe.Fori(1, (NB - 1) // 2) as i:
                b = i * 2 + 1
                attend(b, 1)
                attend(b + 1, 0)
            attend(NB - 1, 1, final=True)
            pe.wait_ge(pT_ready_dve, 2 * NB)
            weigh_v(1, 1)
            pe.wait_ge(pn_ready, NB * NC - 1)
            transpose_p(2)
            pe.wait_ge(pT_ready_act, 2 * NB - 1)
            weigh_v(1, 2)
            pe.wait_ge(pn_ready, NB * NC)
            transpose_p(3)
            pe.wait_ge(rT_ready, 2)
            pe.wait_ge(lt_ready, 1)
            logits(BK)
            pe.wait_ge(rn_ready, 3)
            transpose_r(2, BQ)
            pe.wait_ge(onTl_ready, NB - 1)
            pe.wait_ge(x1_ready, NB - 2)
            project_rows(BY, onTh, onTl, WO, y_done)
            pe.wait_ge(pT_ready_act, 2 * NB)
            weigh_v(1, 3)
            spread(0, 0, first=True)
            pe.wait_ge(onTl_ready, NB)
            pe.wait_ge(x1_ready, NB - 1)
            project_rows(BY, onTh, onTl, WO, y_done)

            def route(b, k4, early=False, left=NB):
                k = k4 % 2
                if left > 2:
                    pe.wait_ge(rT_ready, b + 3)
                    pe.wait_ge(lt_ready, b + 2)
                    logits()
                if left > 3:
                    pe.wait_ge(rn_ready, b + 4)
                    transpose_r((k4 + 3) % 4)
                if left > 1:
                    if early and b == 0:
                        pe.wait_ge(x1_ready, NB)
                    spread(b + 1, 1 - k, first=early and b == 0)
                pe.wait_ge(pm_ready, b + 1)
                pe.wait_ge(rl_ready, b + 1)
                if not early:
                    pe.wait_ge(d_kept, b - 1)
                for h in range(KH):
                    for q, part in enumerate((rh, rl)):
                        last = pe.matmul(BD[k][h][:, :], part[:, k4, h * P:(h + 1) * P],
                                         permb[:, k, :, :].rearrange("p g s -> p (g s)"), start=(q == 0), stop=(q == 1))
                last.then_inc(d_done, 1)

            for b in range(4):
                route(b, b, early=(b < 2))
            with pe.Fori(1, (NB - 4) // 4) as i:
                b = i * 4
                for k4 in range(4):
                    route(b + k4, k4)
            for k4 in range(4):
                route(NB - 4 + k4, k4, left=4 - k4)

            BH, BE = bank[0:2], bank[2:4]

            def expert_in(r):
                k = r % 2
                for s in range(NS):
                    for h in range(KH):
                        last = pe.matmul(BH[k][s * F:(s + 1) * F, 0:GROUPS],
                                         wx[:, r, h * P + s * F:h * P + (s + 1) * F], xe[:, r % XR, h, s, :],
                                         start=(h == 0), stop=(h == KH - 1), tile_position=(0, s * F))
                last.then_inc(h_done, 1)

            def expert_out(r):
                k = r % 2
                for h in range(KH):
                    last = pe.matmul(BE[k][:, h * E:(h + 1) * E], wx[:, r, KH * P + h * P:KH * P + (h + 1) * P],
                                     hb[:, k].rearrange("p s g -> p (s g)"), start=True, stop=True)
                last.then_inc(e_done, 1)

            def expert(e, r, loads):
                if loads is not None:
                    pe.wait_ge(wx_loaded[(r + 1) % RING], loads)
                    pe.wait_ge(xe_ready, e + 2)
                    if r > 0 or not isinstance(e, int):
                        pe.wait_ge(h_ready, e)
                    expert_in((r + 1) % RING)
                pe.wait_ge(h_ready, e + 1)
                if not isinstance(e, int) or e >= 2:
                    pe.wait_ge(e_kept, e - 1)
                expert_out(r)

            pe.wait_ge(d_kept, NB)
            pe.wait_ge(d_kept_dve, 2)
            pe.wait_ge(wx_loaded[0], 16)
            pe.wait_ge(xe_ready, 1)
            expert_in(0)
            for e in range(2):
                expert(e, e, 16)
            with pe.Fori(0, NE // RING - 1) as i:
                for r in range(2, RING + 2):
                    expert(i * RING + r, r % RING, i * 16 + 16 * (1 + (r + 1) // RING))
            for r in range(2, RING):
                expert(NE - RING + r, r, 16 * (NE // RING) if r < RING - 1 else None)

            BY2, BC = (bank[4:6], bank[6:8]), bank[0:2]

            def transpose_y(k):
                for g in range(NG):
                    for h in range(KH):
                        o = (g % 2) * E + h * P
                        last = pe.transpose(BY2[k][g // 2][:, o:o + P], yg[:, k, h, g, :], ident)
                last.then_inc(yT_done, 1)

            def combine(b, k, early=False, final=False):
                if not final:
                    pe.wait_ge(yg_ready, b + 2)
                    if not isinstance(b, int) or b >= 1:
                        pe.wait_ge(ys_ready, b)
                    transpose_y(1 - k)
                pe.wait_ge(ys_ready, b + 1)
                pe.wait_ge(pg_ready, b + 1)
                if not early:
                    pe.wait_ge(yo_ready, b - 1)
                for g in range(NG):
                    last = pe.matmul(BC[k][g * T:(g + 1) * T, 0:E], pg[:, k, g * T:(g + 1) * T],
                                     ys[:, k, g, :], start=True, stop=True, tile_position=(0, g * T))
                last.then_inc(c_done, 1)

            pe.wait_ge(e_kept, NE)
            pe.wait_ge(yg_ready, 1)
            transpose_y(0)
            combine(0, 0, early=True)
            combine(1, 1, early=True)
            with pe.Fori(1, (NB - 2) // 2) as i:
                b = i * 2
                for k in range(2):
                    combine(b + k, k)
            combine(NB - 2, 0)
            combine(NB - 1, 1, final=True)

        @block.scalar
        def _(act):
            act.dma_start(w[:, 0], wattn[:, 0]).then_inc(w_loaded[0], 16)
            act.dma_start(cf[:, :], constf).then_inc(consts_loaded, 16)
            act.dma_start(w[:, 1], wattn[:, 1]).then_inc(w_loaded[1], 16)
            act.wait_ge(act_warm, 1)
            act.activation(warm[:, :], warm[:, :], ACT.Exp)
            act.dma_start(gb[:, :], gbo).then_inc(gates_loaded, 16)
            for i in range(2, 4):
                act.dma_start(w[:, i], wattn[:, i]).then_inc(w_loaded[i], 16)

            def keep_q(k):
                for r in range(2):
                    last = act.activation(qz[64 * r:64 * r + 64, k, :, r, :],
                                          BQ[64 * r:64 * r + 64, 0:E].rearrange("p (h t) -> p h t", h=KH),
                                          ACT.Copy, scale=float(D) ** -0.5)
                last.then_inc(q_ready, 1)

            def keep_v(k):
                act.activation(va[:, k, :, D:2 * D], BK[:, 0:E].rearrange("p (h d) -> p h d", h=H), ACT.Copy)\
                    .then_inc(v_ready, 1)

            def keep_pT(c):
                act.activation(pT[:, c % 2, :], BT[:, :], ACT.Copy).then_inc(pT_ready_act, 1)

            def keep_onT(k):
                act.activation(onTh[:, :, :], BO[k][:, 0:E].rearrange("p (h t) -> p h t", h=KH), ACT.Copy)\
                    .then_inc(onTh_ready, 1)

            def context_high(k):
                act.activation(cTh[:, k], cT[:, k], ACT.Copy).then_inc(c_high, 1)

            def keep_r(of=0):
                act.activation(rT[:, :, :], bank[of][:, 0:E].rearrange("p (h t) -> p h t", h=KH), ACT.Copy)\
                    .then_inc(rT_ready, 1)

            def keep_d(b, k, halves=KH):
                act.wait_ge(d_done, b + 1)
                for h in range(halves):
                    last = act.activation(routed[:, h, bass.ds(b * NG, NG), :],
                                          bank[5 - 2 * k + h][:, :].rearrange("p (g s) -> p g s", g=NG), ACT.Copy)
                last.then_inc(d_kept, 1)

            def rows_high(b, k4):
                act.wait_ge(rn_ready, b + 1)
                act.activation(rh[:, k4], xn[:, k4], ACT.Copy).then_inc(rh_ready, 1)

            def softmax(b, k, loads=None, first=False, second=False, final=False):
                for c in range(NC):
                    n = b * NC + c
                    if not first or c >= 2:
                        act.wait_ge(pT_done, n - 1)
                    if c < 2 and not first:
                        keep_pT(c)
                    act.wait_ge(max_ready, n + 1)
                    for j in range(HC):
                        last = act.activation(pr[:, c % 2, j, :], BS[c % 2][:, j * P:(j + 1) * P], ACT.Exp,
                                              bias=nmax[:, c * HC + j:c * HC + j + 1],
                                              accum_out=psum[:, c * HC + j:c * HC + j + 1])
                    last.then_inc(p_ready, 1)
                    if c == 0 and loads is not None:
                        act.wait_ge(ctx_loaded[k], loads)
                        context_high(k)
                    if c == 2 and not final:
                        act.wait_ge(q_done, b + 2)
                        keep_q(1 - k)
                    if c == 3:
                        if not first:
                            act.wait_ge(av_done, b * NC)
                            if not second:
                                act.wait_ge(y_done, b - 1)
                            keep_onT(1 - k)
                    if final and c >= 1:
                        if c >= 2:
                            act.wait_ge(rT_done, c - 1)
                            keep_r(6)
                        rows_high(c - 1, c - 1)

            for k in range(2):
                act.wait_ge(ctx_loaded[k], 16)
                context_high(k)
            act.wait_ge(gates_loaded, 16)
            act.activation(tg[:, :], gates_sb[:, :], ACT.Tanh).then_inc(tanh_ready, 1)
            act.wait_ge(q_done, 1)
            act.wait_ge(zeroed, 2)
            keep_q(0)
            act.wait_ge(v_done, 1)
            keep_v(0)
            softmax(0, 0, 32, first=True)
            softmax(1, 1, 32, second=True)
            softmax(2, 0, 48)
            with act.Fori(1, NB // 2 - 2) as i:
                b = i * 2 + 1
                for k in range(2):
                    softmax(b + k, 1 - k, i * 16 + (32 + 16 * k))
            softmax(NB - 3, 1, 16 * (NB // 2))
            softmax(NB - 2, 0)
            softmax(NB - 1, 1, final=True)
            act.wait_ge(pT_done, NB * NC - 1)
            keep_pT(0)
            act.wait_ge(pT_done, NB * NC)
            keep_pT(1)
            act.wait_ge(rT_done, 3)
            keep_r(6)
            act.wait_ge(av_done, NB * NC)
            act.wait_ge(y_done, NB - 1)
            keep_onT(1)

            def route(b, k4, left=NB):
                if left > 3:
                    rows_high(b + 3, (k4 + 3) % 4)
                    act.wait_ge(rT_done, b + 4)
                    keep_r()
                keep_d(b, k4 % 2, KH if left > 2 else 1)

            with act.Fori(0, NB // 4 - 1) as i:
                b = i * 4
                for k4 in range(4):
                    route(b + k4, k4)
            for k4 in range(4):
                route(NB - 4 + k4, k4, left=4 - k4)

            with act.Fori(0, NE // 2) as i:
                e = i * 2
                for k in range(2):
                    act.wait_ge(e_done, e + (k + 1))
                    act.activation(routed[:, :, :, bass.ds((e + k) * NS, NS)],
                                   bank[2 + k][:, :].rearrange("p (h s g) -> p h g s", h=KH, s=NS), ACT.Copy)\
                        .then_inc(e_kept, 1)

            with act.Fori(0, NB // 2) as i:
                b = i * 2
                for k in range(2):
                    act.wait_ge(yT_done, b + (k + 1))
                    for q in range(2):
                        last = act.activation(ys[:, k, 2 * q:2 * q + 2, :],
                                              bank[4 + 2 * k + q][:, :].rearrange("p (g e) -> p g e", g=2), ACT.Copy)
                    last.then_inc(ys_ready, 1)

        @block.vector
        def _(dve):
            steps = [0]

            def step(ins):
                steps[0] += 1
                ins.then_inc(dve_step, 1)

            def rstd(stage, lo, hi):
                m, q, v, y, t = mv[:, lo:hi, 0], mv[:, lo:hi, 1], ve[:, lo:hi], rs[:, lo:hi], nt[:, lo:hi]
                if stage > 0:
                    dve.wait_ge(dve_step, steps[0])
                if stage == 0:
                    dve.tensor_tensor(m, stats[:, lo:hi, 1], stats[:, lo:hi, 4], ALU.add)
                    dve.tensor_tensor(q, stats[:, lo:hi, 1], stats[:, lo:hi, 4], ALU.subtract)
                    step(dve.tensor_tensor(v, stats[:, lo:hi, 2], stats[:, lo:hi, 5], ALU.add))
                elif stage == 1:
                    dve.tensor_scalar(m, m, 0.5, None, ALU.mult)
                    dve.tensor_scalar(v, v, 1.0 / E, EPS, ALU.mult, ALU.add)
                    step(dve.tensor_tensor(q, q, q, ALU.mult))
                elif stage == 2:
                    step(dve.scalar_tensor_tensor(v, q, 0.25, v, ALU.mult, ALU.add))
                elif stage == 3:
                    dve.tensor_scalar(y.bitcast(I32), v.bitcast(I32), -0.5, RSQRT_SEED, ALU.mult, ALU.add)
                    step(dve.tensor_scalar(q, v, -0.5, None, ALU.mult))
                elif stage % 3 == 1:
                    step(dve.tensor_tensor(t, q, y, ALU.mult))
                elif stage % 3 == 2:
                    step(dve.tensor_tensor(t, t, y, ALU.mult))
                else:
                    step(dve.scalar_tensor_tensor(y, t, 1.5, y, ALU.add, ALU.mult))

            def rstd_ready():
                dve.wait_ge(dve_step, steps[0])

            def statistics(lo, hi):
                for b in range(lo, hi):
                    if b == lo or b % XC == 0:
                        dve.wait_ge(x_loaded[b // XC], 16)
                    last = dve.bn_stats(stats[:, b, :], xs[:, b, :])
                step(last)

            dve.memset(warm[:, :], 0.0).then_inc(act_warm, 1)
            for c in range(2):
                dve.memset(BS[c][:, :], NEG).then_inc(above_ready, 1)
            statistics(0, XC)
            rstd_ready()
            for stage in range(RSTD_STAGES):
                rstd(stage, 0, XC)
            rstd_ready()

            def split_weight(m):
                dve.wait_ge(w_loaded[2 + m], 16)
                dve.tensor_copy(wh[:, m], w[:, 2 + m]).then_inc(w_high, 1)
                dve.wait_ge(w_high, m + 1)
                dve.tensor_tensor(wl[:, m], w[:, 2 + m], wh[:, m].bitcast(F32), ALU.subtract).then_inc(w_ready, 1)

            def normalize(b, k, ready):
                dve.tensor_scalar(xn[:, k, :], xs[:, b, :], mv[:, b, 0:1], rs[:, bass.ds(b, 1)],
                                  ALU.subtract, ALU.mult).then_inc(ready, 1)

            def keep_k(k, h):
                return dve.tensor_tensor(kd[:, k, h], BK[:, None, h * P:(h + 1) * P].to_broadcast([P, HC, P]),
                                         headmask[:, :, None].to_broadcast([P, HC, P]), ALU.mult)

            def keep_v(k):
                dve.tensor_copy(va[:, k, :, D:2 * D], BK[:, 0:E].rearrange("p (h d) -> p h d", h=H))\
                    .then_inc(v_ready, 1)

            def keep_x(b):
                dve.wait_ge(xT_done, b + 1)
                dve.tensor_copy(xT[:, :, :], XQ.rearrange("p (h t) -> p h t", h=KH)).then_inc(xT_ready, 1)

            def inverse_sums(n, c):
                dve.wait_ge(p_ready, n + 1)
                dve.reciprocal(rsum[:, c * HC:(c + 1) * HC], psum[:, c * HC:(c + 1) * HC]).then_inc(rsum_ready, 1)

            def low_part(b, k):
                dve.wait_ge(onTh_ready, b + 1)
                dve.tensor_tensor(onTl[:, :, :], BO[k][:, 0:E].rearrange("p (h t) -> p h t", h=KH),
                                  onTh[:, :, :].bitcast(F32), ALU.subtract).then_inc(onTl_ready, 1)

            def residual(b):
                dve.scalar_tensor_tensor(xs[:, b, :], BY[:, 0:E], tg[:, 0:1], xs[:, b, :], ALU.mult, ALU.add)\
                    .then_inc(x1_ready, 1)

            def keep_pT(c):
                dve.tensor_copy(pT[:, c % 2, :], BT[:, :]).then_inc(pT_ready_dve, 1)

            lg = lt[:, :].rearrange("p (g t) -> p g t", g=NG)

            def add_ramp(b, of=1):
                if not isinstance(b, int) or b > 0:
                    dve.wait_ge(perm_ready, b)
                dve.wait_ge(lg_done, b + 1)
                dve.tensor_tensor(lt[:, :], bank[of][:, 0:P], tie, ALU.add).then_inc(lt_ready, 1)

            def pick(b, k, early):
                dve.wait_ge(lt_ready, b + 1)
                dve.tensor_reduce(gmax[:, :], lg, AX_X, ALU.max).then_inc(gmax_ready, 1)
                dve.wait_ge(gmax_ready, b + 1)
                if not early:
                    dve.wait_ge(permT_kept, b - 1)
                dve.tensor_tensor(pc[:, k, :].rearrange("p (g t) -> p g t", g=NG), lg,
                                  gmax[:, :, None].to_broadcast([P, NG, T]), ALU.is_equal).then_inc(perm_ready, 1)

            def spread(b, k):
                dve.wait_ge(pm_done, b + 1)
                dve.tensor_tensor(permb[:, k, :, :], bank[(2, 7)[k]][:, None, 0:P].to_broadcast([P, NG, P]),
                                  groupmask[:, :, None].to_broadcast([P, NG, P]), ALU.mult).then_inc(pm_ready, 1)

            def attend(b, k, first=False, second=False, final=False, rows=None):
                late = not first and not second
                for c in range(NC):
                    n = b * NC + c
                    if c == 3 and rows is None:
                        inverse_sums(n - 1, c - 1)
                    dve.wait_ge(s_done, n + 1)
                    dve.tensor_reduce(nmax[:, c * HC:(c + 1) * HC], BS[c % 2][:, :].rearrange("p (j t) -> p j t", j=HC),
                                      AX_X, ALU.max, negate=True).then_inc(max_ready, 1)
                    if rows is not None:
                        rstd(3 * c, *rows)
                    if (not first or c >= 1) and not (c == 3 and rows is None):
                        inverse_sums(n - 1, (c - 1) % NC)
                    if rows is not None:
                        rstd(3 * c + 1, *rows)
                    if c == 0 and late:
                        low_part(b - 2, k)
                    if c >= 2:
                        dve.wait_ge(pT_done, n - 1)
                        keep_pT(c)
                    if c == 0 and not final and not first:
                        normalize(b + 1, 0, xn_ready)
                    if c == 0 and not final:
                        dve.wait_ge(k_done, b + 2)
                        keep_k(1 - k, 0)
                    if c == 1 and not final:
                        keep_k(1 - k, 1).then_inc(k_ready, 1)
                        keep_x(b + 1)
                    if rows is not None:
                        rstd(3 * c + 2, *rows)
                    if first:
                        statistics(XC + c, XC + c + 1)
                    if second:
                        statistics(2 * XC + 2 * c, 2 * XC + 2 * (c + 1))
                    if c == 2 and late:
                        dve.wait_ge(y_done, b - 1)
                        dve.wait_ge(xb_ready, b - 1)
                        residual(b - 2)
                        dve.wait_ge(x1_ready, b - 1)
                        dve.bn_stats(stats[:, b - 2, :], xs[:, b - 2, :]).then_inc(stats_ready, 1)
                    if c == 3 and rows is not None:
                        rstd(RSTD_STAGES - 1, *rows)
                    if final:
                        normalize(c, c, rn_ready)
                    if c == 3 and not final:
                        dve.wait_ge(v_done, b + 2)
                        keep_v(1 - k)

            normalize(0, 0, xn_ready)
            dve.wait_ge(consts_loaded, 16)
            dve.wait_ge(k_done, 1)
            keep_k(0, 0)
            keep_k(0, 1).then_inc(k_ready, 1)
            keep_x(0)
            split_weight(0)
            normalize(1, 0, xn_ready)
            dve.wait_ge(gates_loaded, 16)
            dve.wait_ge(tanh_ready, 1)
            dve.tensor_scalar(bo_sb[:, :], bo_sb[:, :], tg[:, 0:1], None, ALU.mult).then_inc(bo_ready, 1)
            split_weight(1)
            attend(0, 0, first=True)
            rstd_ready()
            attend(1, 1, second=True, rows=(XC, 2 * XC))
            rstd_ready()
            attend(2, 0)
            attend(3, 1, rows=(2 * XC, NB))
            rstd_ready()
            with dve.Fori(2, (NB - 2) // 2) as i:
                b = i * 2
                for k in range(2):
                    attend(b + k, k)
            def route(b, k4, early=False, left=NB, stages=()):
                for stage in stages[:2]:
                    rstd(stage, NB - 4, NB)
                if left > 2:
                    add_ramp(b + 2)
                if left > 4:
                    dve.wait_ge(rl_ready, b + 1)
                    normalize(b + 4, k4, rn_ready)
                for stage in stages[2:]:
                    rstd(stage, NB - 4, NB)
                if left > 2:
                    pick(b + 2, k4 % 2, early)
                if left > 1:
                    spread(b + 1, (k4 + 1) % 2)

            dve.wait_ge(stats_ready, NB - 4)
            attend(NB - 2, 0, rows=(0, NB - 4))
            rstd_ready()
            attend(NB - 1, 1, final=True)

            def finish_attention(b):
                dve.wait_ge(y_done, b + 1)
                dve.wait_ge(xb_ready, b + 1)
                residual(b)
                dve.wait_ge(x1_ready, b + 1)
                dve.bn_stats(stats[:, b, :], xs[:, b, :]).then_inc(stats_ready, 1)

            inverse_sums(NB * NC - 1, NC - 1)
            low_part(NB - 2, 0)
            add_ramp(0, 5)
            pick(0, 0, True)
            finish_attention(NB - 2)
            add_ramp(1, 5)
            pick(1, 1, True)
            low_part(NB - 1, 1)
            spread(0, 0)
            finish_attention(NB - 1)
            dve.wait_ge(stats_ready, NB)
            for b in range(4):
                route(b, b, stages=range(4 * b, min(4 * b + 4, RSTD_STAGES)))
            rstd_ready()
            with dve.Fori(1, (NB - 4) // 4) as i:
                b = i * 4
                for k4 in range(4):
                    route(b + k4, k4)
            for k4 in range(4):
                route(NB - 4 + k4, k4, left=4 - k4)

            for b in range(NB - 2, NB):
                dve.wait_ge(d_done, b + 1)
                dve.tensor_copy(routed[:, 1, b * NG:(b + 1) * NG, :],
                                bank[6 - 2 * (b % 2)][:, :].rearrange("p (g s) -> p g s", g=NG))\
                    .then_inc(d_kept_dve, 1)

            def stage(e, k):
                dve.tensor_copy(xe[:, k].rearrange("p h s g -> p h g s"),
                                routed[:, :, :, bass.ds(e * NS, NS)]).then_inc(xe_ready, 1)

            def hidden(e, r, loads, early=False, left=NE):
                k = r % 2
                if not early:
                    dve.wait_ge(e_done, e - 1)
                dve.wait_ge(wx_loaded[r], loads)
                dve.wait_ge(h_done, e + 1)
                for s in range(NS):
                    q = slice(s * F, (s + 1) * F)
                    last = dve.tensor_scalar(hb[q, k, s, :], bank[k][q, 0:GROUPS], wx[q, r, KH * P + E:],
                                             0.0, ALU.add, ALU.max)
                last.then_inc(h_ready, 1)
                if left > XR - 1:
                    stage(e + XR - 1, (r + XR - 1) % XR)

            dve.wait_ge(d_kept, NB)
            dve.wait_ge(d_kept_dve, 2)
            for e in range(XR - 1):
                stage(e, e)
            dve.wait_ge(zeroed, 3)
            for e in range(2):
                hidden(e, e, 16, early=True)
            with dve.Fori(0, NE // RING - 1) as i:
                for r in range(2, RING + 2):
                    hidden(i * RING + r, r % RING, i * 16 + 16 * (1 + r // RING))
            for r in range(2, RING):
                hidden(NE - RING + r, r, 16 * (NE // RING), left=RING - r)

            def stage_y(b, k):
                dve.tensor_copy(yg[:, k], routed[:, :, bass.ds(b * NG, NG), :]).then_inc(yg_ready, 1)

            def finish(b, k):
                dve.wait_ge(c_done, b + 1)
                dve.scalar_tensor_tensor(xs[:, b, :], bank[k][:, 0:E], tg[:, 1:2], xs[:, b, :], ALU.mult, ALU.add)\
                    .then_inc(yo_ready, 1)

            dve.wait_ge(e_kept, NE)
            stage_y(0, 0)
            stage_y(1, 1)
            dve.wait_ge(yT_done, 1)
            stage_y(2, 0)
            with dve.Fori(0, NB // 2 - 2) as i:
                b = i * 2
                for k in range(2):
                    dve.wait_ge(yT_done, b + (k + 2))
                    stage_y(b + (k + 3), 1 - k)
                    finish(b + k, k)
            dve.wait_ge(yT_done, NB - 2)
            stage_y(NB - 1, 1)
            for b in range(NB - 4, NB):
                finish(b, b % 2)


def constants():
    import numpy as np

    rows = np.arange(P)
    ident = np.eye(P, dtype=np.float32)
    heads = ((rows[:, None] // D) % HC == np.arange(HC)[None, :]).astype(np.float32)
    step = np.arange(T, dtype=np.float32) * (np.float32(1e-6) / np.float32(T - 1))
    ramp = np.broadcast_to(np.tile(step, NG)[None, :], (P, P))
    groups = (rows[:, None] // T == np.arange(NG)[None, :]).astype(np.float32)
    mask = np.where(np.arange(DP)[None, :] <= rows[:, None] % DP, 0.0, NEG).astype(np.float32)
    return np.concatenate([ident, heads, ramp, groups, mask], axis=1)


def kernel(**inputs):
    import numpy as _np
    import concourse.bacc as _bacc
    from concourse import mybir as _mybir
    from concourse.bass_utils import run_bass_kernel_spmd as _run

    a = {name: _np.asarray(v) for name, v in inputs.items()}

    def halves(m):
        return m.reshape(KH, P, -1).transpose(1, 0, 2)

    wo = a["L0_xattn_Wo"].T.reshape(KH, NC // KH, HC, D, E).transpose(0, 2, 1, 3, 4).reshape(E, E)
    f1 = a["L0_ffn_f1"].reshape(KH, P, NE, NS * F).transpose(2, 1, 0, 3).reshape(NE, P, KH * NS * F)
    f2 = a["L0_ffn_f2"].reshape(NE, NS * F, E)
    laid = {
        "x": a["x"],
        "ctxT": a["ctx_1024"].reshape(NB, P, KH, P).transpose(0, 3, 2, 1),
        "wattn": _np.stack([halves(m) for m in [a["L0_xattn_" + n].T for n in ("Wk", "Wq", "Wv")] + [wo]], axis=1),
        "gbo": _np.broadcast_to(_np.concatenate([a["g_xattn"], a["g_ffn"], a["L0_xattn_bo"]]), (P, 2 + E)),
        "ctrl": halves(a["L0_ffn_controller"].reshape(E, SLOTS)),
        "wexp": _np.concatenate([f1, f2, a["L0_ffn_bias"].reshape(NE, NS * F, 1)], axis=2),
        "constf": constants(),
    }
    nc = _bacc.Bacc("TRN2", target_bir_lowering=False, num_devices=1)
    arrays, args = {}, []
    for name, v in laid.items():
        v = _np.ascontiguousarray(v)
        arrays[f"in_{name}_dram"] = v
        args.append(nc.dram_tensor(f"in_{name}_dram", v.shape, _mybir.dt.from_np(v.dtype), kind="ExternalInput").ap())
    args.append(nc.dram_tensor("out_0_dram", (NB, P, E), F32, kind="ExternalOutput").ap())
    build(nc, *args)
    r = _run(nc, [arrays], core_ids=[0])
    return r.results[0]["out_0_dram"]
```
